# Optimizing a Trainium2 kernel written in Bass

```python
import numpy as np
import jax
import jax.numpy as jnp

def _softmax(x, axis=-1):
    return jax.nn.softmax(x, axis=axis)

def _gelu(x):
    return jax.nn.gelu(x, approximate=True)

def _silu(x):
    return jax.nn.silu(x)

def _sigmoid(x):
    return jax.nn.sigmoid(x)

def _layernorm(x, axis=-1, eps=1e-05):
    m = jnp.mean(x, axis=axis, keepdims=True)
    v = jnp.var(x, axis=axis, keepdims=True)
    return (x - m) / jnp.sqrt(v + eps)

def _scatter_add(tgt, idx, src, axis=0):
    return tgt.at[idx].add(src)

def _segment_sum(src, seg, n):
    return jax.ops.segment_sum(src, seg, n)
kernel_name = 'mk_seq_preln_d1_jaxref_r8_b5619e'

def setup_inputs(seed: int=0):
    np.random.seed(seed)
    _w = jnp.asarray

    def _L0_attn_setup():
        import jax, jax.numpy as jnp
        import numpy as np
        NUM_HEADS = 16
        key = jax.random.key(seed)
        ks = jax.random.split(key, 9)
        B, S, D = (2, 256, 256)
        scale = 1.0 / np.sqrt(D).astype(np.float32)
        x = jax.random.normal(ks[0], (B, S, D), jnp.float32)
        wq = jax.random.normal(ks[1], (D, D), jnp.float32) * scale
        wk = jax.random.normal(ks[2], (D, D), jnp.float32) * scale
        wv = jax.random.normal(ks[3], (D, D), jnp.float32) * scale
        wo = jax.random.normal(ks[4], (D, D), jnp.float32) * scale
        bq = jax.random.normal(ks[5], (D,), jnp.float32) * 0.02
        bk = jax.random.normal(ks[6], (D,), jnp.float32) * 0.02
        bv = jax.random.normal(ks[7], (D,), jnp.float32) * 0.02
        bo = jax.random.normal(ks[8], (D,), jnp.float32) * 0.02
        return {'x': x, 'wq': wq, 'bq': bq, 'wk': wk, 'bk': bk, 'wv': wv, 'bv': bv, 'wo': wo, 'bo': bo}
    _L0_attn_in = _L0_attn_setup()

    def _L0_ffn_setup():
        import jax, jax.numpy as jnp
        import numpy as np
        NUM_EXPERTS = 64
        TOP_K = 8
        HIDDEN = 256
        INTER = 128
        key = jax.random.key(seed)
        k1, k2, k3, k4 = jax.random.split(key, 4)
        scale = 1.0 / np.sqrt(HIDDEN)
        hidden_states = jax.random.normal(k1, (4, 256, HIDDEN), dtype=jnp.float32)
        gate_w = jax.random.normal(k2, (NUM_EXPERTS, HIDDEN), dtype=jnp.float32) * scale
        w13 = jax.random.normal(k3, (NUM_EXPERTS, 2 * INTER, HIDDEN), dtype=jnp.float32) * scale
        w2 = jax.random.normal(k4, (NUM_EXPERTS, HIDDEN, INTER), dtype=jnp.float32) * (1.0 / np.sqrt(INTER))
        return {'hidden_states': hidden_states, 'gate_w': gate_w, 'w13': w13, 'w2': w2}
    _L0_ffn_in = _L0_ffn_setup()
    _d = {'L0_attn_x': _L0_attn_in['x'], 'L0_attn_wq': _L0_attn_in['wq'], 'L0_attn_bq': _L0_attn_in['bq'], 'L0_attn_wk': _L0_attn_in['wk'], 'L0_attn_bk': _L0_attn_in['bk'], 'L0_attn_wv': _L0_attn_in['wv'], 'L0_attn_bv': _L0_attn_in['bv'], 'L0_attn_wo': _L0_attn_in['wo'], 'L0_attn_bo': _L0_attn_in['bo'], 'L0_ffn_gate_w': _L0_ffn_in['gate_w'], 'L0_ffn_w13': _L0_ffn_in['w13'], 'L0_ffn_w2': _L0_ffn_in['w2']}
    _x0 = _d['L0_attn_x']
    _d['L0_attn_x'] = jax.random.normal(jax.random.fold_in(jax.random.key(seed), 1), (8, 256, 256), dtype=_x0.dtype)
    del _x0
    return _d

def reference(L0_attn_x, L0_attn_wq, L0_attn_bq, L0_attn_wk, L0_attn_bk, L0_attn_wv, L0_attn_bv, L0_attn_wo, L0_attn_bo, L0_ffn_gate_w, L0_ffn_w13, L0_ffn_w2):

    def _L0_attn_ref(x, wq, bq, wk, bk, wv, bv, wo, bo):
        import jax, jax.numpy as jnp
        import numpy as np
        NUM_HEADS = 16
        B, S, D = x.shape
        H = NUM_HEADS
        hd = D // H
        inv_sqrt_hd = jnp.float32(1.0 / np.sqrt(hd))
        q = (x @ wq.T + bq).reshape(B, S, H, hd)
        k = (x @ wk.T + bk).reshape(B, S, H, hd)
        v = (x @ wv.T + bv).reshape(B, S, H, hd)
        scores = jnp.einsum('bqhd,bkhd->bhqk', q, k) * inv_sqrt_hd
        causal = jnp.triu(jnp.ones((S, S), dtype=bool), k=1)
        scores = jnp.where(causal[None, None, :, :], -jnp.inf, scores)
        probs = jax.nn.softmax(scores, axis=-1)
        attn = jnp.einsum('bhqk,bkhd->bqhd', probs, v).reshape(B, S, D)
        return attn @ wo.T + bo

    def _L0_ffn_ref(hidden_states, gate_w, w13, w2):
        import jax, jax.numpy as jnp
        import numpy as np
        NUM_EXPERTS = 64
        TOP_K = 8
        HIDDEN = 256
        INTER = 128
        orig_shape = hidden_states.shape
        x = hidden_states.reshape(-1, HIDDEN)
        logits = jnp.einsum('th,eh->te', x, gate_w)
        probs = jax.nn.softmax(logits, axis=-1)
        topk_w, topk_idx = jax.lax.top_k(probs, TOP_K)
        combine = (jax.nn.one_hot(topk_idx, NUM_EXPERTS, dtype=x.dtype) * topk_w[..., None]).sum(axis=1)

        def step(acc, inp):
            w13_e, w2_e, c = inp
            g = x @ w13_e[:INTER].T
            u = x @ w13_e[INTER:].T
            h = jax.nn.silu(g) * u
            o = h @ w2_e.T
            return (acc + c[:, None] * o, None)
        out0 = jnp.zeros_like(x)
        out, _ = jax.lax.scan(step, out0, (w13, w2, combine.T))
        return out.reshape(orig_shape)
    x = L0_attn_x
    x = x + _L0_attn_ref(_layernorm(x, axis=-1), L0_attn_wq, L0_attn_bq, L0_attn_wk, L0_attn_bk, L0_attn_wv, L0_attn_bv, L0_attn_wo, L0_attn_bo)
    x = x + _L0_ffn_ref(_layernorm(x, axis=-1), L0_ffn_gate_w, L0_ffn_w13, L0_ffn_w2)
    return x

_drawn_inputs = setup_inputs


def setup_inputs(seed=0):
    import zlib

    import numpy as np

    out = dict(_drawn_inputs(seed))
    spreads = {}
    factors = {'L0_attn_bq': 8.0, 'L0_attn_bk': 8.0, 'L0_attn_bv': 2.694, 'L0_attn_bo': 2.777}
    for name, (base, spread) in spreads.items():
        noise = np.random.default_rng([zlib.crc32(name.encode()), seed]).standard_normal(out[name].shape)
        drawn = base * np.exp(spread * noise) if base else spread * noise
        out[name] = jnp.asarray(drawn.astype(out[name].dtype))
    for name, factor in factors.items():
        out[name] = (out[name] * factor).astype(out[name].dtype)
    return out
```

```python
import numpy as np
import concourse.bass as bass
from concourse import mybir
from contextlib import ExitStack

NB, SEQ, D = 8, 256, 256
NH, HD = 16, 16
NE, TOPK, INTER = 64, 8, 128
P = 128
T = NB * SEQ
NT = T // P
QT = SEQ // P
DC = D // P
PAIRS = NH // 2
VW = HD + 1
CAPT = 3
CAP = CAPT * P
REG = T + P
IDC, PRC = D, D + 1
RW = D + 1 + NE
DUMMY = CAP
WW = DC * 2 * INTER + D
EPS = 1e-5
SCALE = float(HD) ** -0.5
LOW = -1e30
RSQRT_MAGIC = 0x5F3759DF
NEWTON = 3
LN_LINKS = 5 + 3 * NEWTON
OVT = (T - CAP) // P
MAX_OVER = 112
LOOP_B = (2, 6)
C_ID, C_LT, C_CAUSAL, C_BASE, C_EVEN, C_ODD, C_EIDX, C_IOTA, C_THR, C_END = (
    np.cumsum([0, P, P, P, NE, 1, 1, NE, 1, OVT]).tolist())


def program(nc, x, wq, wk, wv, wo, bqk, bv, bo, gate, experts, consts, ids, y):
    fp32, bf16, i32 = mybir.dt.float32, mybir.dt.bfloat16, mybir.dt.int32
    ALU, ACT, AX = mybir.AluOpType, mybir.ActivationFunctionType, mybir.AxisListType

    routed = nc.dram_tensor("routed", [NE * REG, RW], fp32, kind="Internal").ap()
    acc = [nc.dram_tensor(f"acc{i}", [T + DUMMY, D], fp32, kind="Internal").ap() for i in range(2)]
    over_table = nc.dram_tensor("over_table", [P, 4], i32, kind="Internal").ap()

    ctx = ExitStack()
    with ctx:
        def sb(name, shape, dt=fp32):
            return ctx.enter_context(nc.sbuf_tensor(name, shape, dt))

        def sem(name):
            return ctx.enter_context(nc.semaphore(name))

        bank = [ctx.enter_context(nc.psum_tensor(f"bank{i}", [P, 512], fp32)) for i in range(8)]
        ps_s1, ps_s0, ps_t1, ps_t0, ps_o0, ps_o1, ps_x0, ps_x1 = bank
        ps_tx, ps_g, ps_u, ps_oa, ps_ob = (bank[0], bank[1]), bank[2], bank[3], (bank[4], bank[6]), (bank[5], bank[7])

        cst = sb("cst", [P, C_END])
        idt = sb("idt", [P, CAPT + NT], i32)
        ident = cst[:, C_ID:C_ID + P]
        ident_b = sb("ident_b", [P, P], bf16)
        before_b = sb("before_b", [P, P], bf16)
        causal_b = sb("causal_b", [P, P], bf16)
        ones_b = sb("ones_b", [P, P], bf16)
        wqs, wks, wvs, wos = (sb(n, [P, DC, D]) for n in ("wqs", "wks", "wvs", "wos"))
        gates = sb("gates", [P, DC, NE])
        bqks = sb("bqks", [P, 2 * DC])
        bkm = sb("bkm", [P, 2, DC])
        bvs = sb("bvs", [P, D])
        bos = sb("bos", [P, D])
        pad_rows = sb("pad_rows", [P, CAPT, RW])
        xall = sb("xall", [P, NT, D])
        xn = sb("xn", [P, QT, D])
        xnT = sb("xnT", [P, DC, SEQ])
        qT = [sb(f"qT{i}", [P, DC, SEQ]) for i in range(2)]
        kT = [sb(f"kT{i}", [P, DC, 2, SEQ]) for i in range(2)]
        vt = [sb(f"vt{i}", [P, QT, NH, VW]) for i in range(2)]
        mx = sb("mx", [P, 2, 4])
        nm = sb("nm", [P, 2, 4])
        pr1 = [sb(f"pr1_{i}", [P, 2, SEQ]) for i in range(2)]
        pr0 = [sb(f"pr0_{i}", [P, 2, P]) for i in range(2)]
        pt1 = [sb(f"pt1_{i}", [P, 4, P]) for i in range(2)]
        pt0 = [sb(f"pt0_{i}", [P, 2, P]) for i in range(2)]
        rden = sb("rden", [P, QT, NH])
        attn = sb("attn", [P, QT, D])
        aT = sb("aT", [P, DC, SEQ])
        xn2 = sb("xn2", [P, QT, D])
        x2T = sb("x2T", [P, DC, SEQ])
        ln = [{n: sb(f"{n}_{i}", s, t) for n, s, t in (
            ("stats", [P, QT, 6], fp32), ("mv", [P, QT, 2], fp32), ("ve", [P, QT], fp32),
            ("half", [P, QT], fp32), ("sh", [P, QT], i32), ("r", [P, QT], fp32), ("t", [P, QT], fp32))}
            for i in range(2)]
        rows = sb("rows", [P, NT, RW])
        lg = sb("lg", [P, QT, NE])
        top = sb("top", [P, QT, TOPK])
        rest = sb("rest", [P, QT, NE])
        chosen = sb("chosen", [P, QT, NE], bf16)
        seen = sb("seen", [P, NE], bf16)
        nmx = sb("nmx", [P, QT])
        elg = sb("elg", [P, QT, NE])
        esum = sb("esum", [P, QT])
        erec = sb("erec", [P, QT])
        place = sb("place", [P, QT, NE])
        slotf = sb("slotf", [P, QT, TOPK])
        slots = sb("slots", [P, NT, TOPK], i32)
        cnt = sb("cnt", [P, NE])
        gt = sb("gt", [P, NE, OVT])
        nov = sb("nov", [P, NE])
        onese = sb("onese", [P, NE])
        cum = sb("cum", [P, NE])
        ge = sb("ge", [P, NE])
        eq = sb("eq", [P, NE])
        ovv = sb("ovv", [P, 8])
        ovi = sb("ovi", [P, 4], i32)
        wexp = [sb(f"wexp{i}", [P, WW]) for i in range(4)]
        xt = [sb(f"xt{i}", [P, CAPT, RW]) for i in range(4)]
        xT = [sb(f"xT{i}", [P, DC, CAP]) for i in range(2)]
        sg = [sb(f"sg{i}", [P, CAP]) for i in range(2)]
        hT = [sb(f"hT{i}", [P, CAP]) for i in range(2)]
        osb = [sb(f"osb{i}", [P, CAPT, D]) for i in range(2)]

        s_x0, s_xrest, s_w, s_cst = sem("x_first"), sem("x_rest"), sem("weights_in"), sem("consts_in")
        pad_link, s_held = sem("pad_link"), sem("wait_held")
        s_prep, s_padrow, s_bkm = sem("consts_ready"), sem("pad_row_ready"), sem("key_bias_ready")
        xn_ready, xnT_ps, xnT_ready = sem("xn_ready"), sem("xnT_ps"), sem("xnT_ready")
        q_ps, k_ps, v_ps = sem("q_ps"), sem("k_ps"), sem("v_ps")
        q_ready, k_ready, v_ready = sem("q_ready"), sem("k_ready"), sem("v_ready")
        s1_done, s0_done = sem("s1_done"), sem("s0_done")
        mx_link, nm1_ready, nm0_ready = sem("mx_link"), sem("nm1_ready"), sem("nm0_ready")
        p1_ready, p0_ready = sem("p1_ready"), sem("p0_ready")
        t1_done, t0_done = sem("t1_done"), sem("t0_done")
        pt1_ready, pt0_ready, av_done = sem("pt1_ready"), sem("pt0_ready"), sem("av_done")
        norm_link, attn_ready, aT_ps, aT_ready = sem("norm_link"), sem("attn_ready"), sem("aT_ps"), sem("aT_ready")
        wo_ps, x2_link, x2_ready = sem("wo_ps"), sem("x2_link"), sem("x2_ready")
        ln_link = [sem("ln1_link"), sem("ln2_link")]
        xn2_ready, x2T_ps, x2T_ready = sem("xn2_ready"), sem("x2T_ps"), sem("x2T_ready")
        lg_ps, lg_read, top_link, mask_ready = sem("lg_ps"), sem("lg_read"), sem("top_link"), sem("mask_ready")
        e_ready, pr_link, probs_ready, rowx_ready = sem("e_ready"), sem("pr_link"), sem("probs_ready"), sem("rowx_ready")
        rank_ps, rank_read, sl_link, slots_ready = sem("rank_ps"), sem("rank_read"), sem("sl_link"), sem("slots_ready")
        prefill_done, scatter_done, acc_init = sem("prefill_done"), sem("scatter_done"), sem("acc_init")
        cnt_ps, ov_link, ov_ready, ov_stored = sem("cnt_ps"), sem("ov_link"), sem("ov_ready"), sem("ov_stored")
        w_in = [sem(f"w_in{i}") for i in range(4)]
        xt_in = [sem(f"xt_in{i}") for i in range(4)]
        tx_ps = [sem("tx0_ps"), sem("tx1_ps")]
        xT_ready = [sem("xT0_ready"), sem("xT1_ready")]
        g_ps, u_ps, sg_ready, h_ready = sem("g_ps"), sem("u_ps"), sem("sg_ready"), sem("h_ready")
        oa_ps, ob_ps, oa_out, ob_out = sem("oa_ps"), sem("ob_ps"), sem("oa_out"), sem("ob_out")
        added = [sem("added0"), sem("added1")]
        v_pad, v_ld, v_tx, v_xT, v_gu, v_sg, v_h = (sem("v_" + n) for n in ("pad", "ld", "tx", "xT", "gu", "sg", "h"))
        v_o, v_osb, v_add = sem("v_o"), sem("v_osb"), sem("v_add")
        f_in, f_sum, f_out = [sem(f"f_in{i}") for i in range(4)], sem("f_sum"), sem("f_out")

        block = ctx.enter_context(nc.Block())

        def wait(eng, s, value):
            if not isinstance(value, int) or value > 0:
                eng.wait_ge(s, value)

        def carry_wait(eng):
            eng.sem_inc(s_held, 1)

        def batches(eng, step):
            lo, hi = LOOP_B
            for b in range(lo):
                step(b, b % 2, b)
            with eng.Fori(0, (hi - lo) // 2) as i:
                step(i * 2 + lo, 0, lo)
                step(i * 2 + lo + 1, 1, lo)
            for b in range(hi, NB + 2):
                step(b, b % 2, b)

        def expert_loop(eng, step):
            for k in range(4):
                step(0, k, k)
            with eng.Fori(1, NE // 4 - 1) as q:
                for k in range(4):
                    step(q, k, 4 + k)
            for e in range(NE - 4, NE + 1):
                step(e // 4, e % 4, e)

        def before(q, k):
            return (q, k - 1) if k else (q - 1, 3)

        def after(q, k):
            return (q, k + 1) if k < 3 else (q + 1, 0)

        def earlier_adds(q, k):
            return (q * 2 + k // 2) * (16 * CAPT)

        def unit(b, s):
            return b * PAIRS + s

        @block.sync
        def _(sp):
            sp.dma_start(xall[:, 0:QT, :], x[0:SEQ, :].rearrange("(t p) d -> p t d", p=P)).then_inc(s_x0, 16)
            sp.dma_start(cst[:, :], consts).then_inc(s_cst, 16)
            sp.dma_start(idt[:, :], ids).then_inc(s_cst, 16)
            for dst, src in ((wqs, wq), (wks, wk), (wvs, wv), (wos, wo), (gates, gate)):
                sp.dma_start(dst[:, :, :], src.rearrange("(c p) o -> p c o", p=P)).then_inc(s_w, 16)
            sp.dma_start(bqks[:, :], bqk).then_inc(s_w, 16)
            sp.dma_start(bvs[:, :], bv.broadcast_to([P, D])).then_inc(s_w, 16)
            sp.dma_start(bos[:, :], bo.broadcast_to([P, D])).then_inc(s_w, 16)
            sp.dma_start(xall[:, QT:NT, :], x[SEQ:T, :].rearrange("(t p) d -> p t d", p=P)).then_inc(s_xrest, 16)
            sp.wait_ge(s_padrow, 1)
            with sp.Fori(0, NE) as e:
                sp.dma_start(routed[bass.ds(e * REG, CAP), :].rearrange("(t p) d -> p t d", p=P),
                             pad_rows[:, :, :]).then_inc(prefill_done, 16)
            for t in range(T // CAP + 1):
                n = min(CAP, T - t * CAP) // P
                sp.dma_start(acc[1][t * CAP:t * CAP + n * P, :].rearrange("(t p) d -> p t d", p=P),
                             pad_rows[:, 0:n, 0:D]).then_inc(acc_init, 16)
            for a in acc:
                sp.dma_start(a[T:T + DUMMY, :].rearrange("(t p) d -> p t d", p=P),
                             pad_rows[:, :, 0:D]).then_inc(acc_init, 16)
            for e in range(4):
                sp.dma_start(wexp[e][:, :], experts[e]).then_inc(w_in[e], 16)
            with sp.Fori(0, NB) as b:
                at = sp.snap(b * SEQ)
                tile = sp.snap(b * QT)
                sp.wait_ge(x2_ready, b + 1)
                sp.dma_start(acc[0][bass.ds(at, SEQ), :].rearrange("(t p) d -> p t d", p=P),
                             xall[:, bass.ds(tile, QT), :]).then_inc(acc_init, 16)
            sp.wait_ge(ov_ready, 1)
            sp.dma_start(over_table, ovi[:, :]).then_inc(ov_stored, 16)
            sp.wait_ge(scatter_done, 16 * NT * TOPK)
            for e in range(4):
                sp.dma_start(xt[e][:, :, :], routed[e * REG:e * REG + CAP, :].rearrange("(t p) d -> p t d", p=P))\
                    .then_inc(xt_in[e], 16)

            with sp.Fori(1, NE // 4) as q:
                for k in range(4):
                    row, wrow = sp.snap((q * 4 + k) * REG), sp.snap((q * 4 + k) * P)
                    used, reuse = sp.snap(q * 4 + (k - 3)), sp.snap(earlier_adds(q - 1, k) + 16 * CAPT)
                    sp.wait_ge(ob_ps, used)
                    sp.dma_start(wexp[k][:, :], experts.rearrange("e p w -> (e p) w")[bass.ds(wrow, P), :])\
                        .then_inc(w_in[k], 16)
                    sp.wait_ge(added[k % 2], reuse)
                    sp.dma_start(xt[k][:, :, :], routed[bass.ds(row, CAP), :].rearrange("(t p) d -> p t d", p=P))\
                        .then_inc(xt_in[k], 16)
            sp.wait_ge(ov_stored, 16)
            total = sp.value_load(over_table[0:1, 3:4], min_val=0, max_val=MAX_OVER)
            for k in range(2):
                sp.wait_ge(added[k], 16 * CAPT * NE // 2)
            with sp.If(total > 0):
                with sp.Fori(0, total) as t:
                    row = sp.value_load(over_table[bass.ds(t, 1), 0:1], min_val=0, max_val=NE * REG - P)
                    e = sp.value_load(over_table[bass.ds(t, 1), 1:2], min_val=0, max_val=NE - 1)
                    pad = sp.value_load(over_table[bass.ds(t, 1), 2:3], min_val=0, max_val=NE * REG - P)
                    sp.dma_start(routed[bass.ds(pad, P), :], pad_rows[:, 0, :]).then_inc(v_pad, 16)
                    sp.dma_start(wexp[0][:, :], experts[bass.ds(e, 1)].rearrange("e p w -> (e p) w")).then_inc(v_ld, 16)
                    src, padded = routed[bass.ds(row, P), :], sp.snap(t * 16 + 16)
                    sp.wait_ge(v_pad, padded)
                    sp.dma_start(xt[0][:, 0, :], src).then_inc(v_ld, 16)
                    sp.wait_ge(v_add, t * 16 + 16)
                    carry_wait(sp)
            for c in range(4):
                n, r = NT // 4, T // 4
                for a in range(2):
                    dst = xall if a == 0 else rows
                    sp.dma_start(dst[:, n * c:n * c + n, 0:D],
                                 acc[a][r * c:r * c + r, :].rearrange("(t p) d -> p t d", p=P)).then_inc(f_in[c], 16)
            for c in range(4):
                sp.wait_ge(f_sum, c + 1)
                sp.dma_start(y[r * c:r * c + r, :].rearrange("(t p) d -> p t d", p=P),
                             xall[:, n * c:n * c + n, :]).then_inc(f_out, 16)
            sp.wait_ge(f_out, 64)
            sp.wait_ge(acc_init, 16 * (T // CAP + 1 + 2 + NB))

        @block.gpsimd
        def _(pool):
            pool.wait_ge(prefill_done, 16 * NE)
            for t in range(NT):
                if t % QT == 0:
                    b = t // QT
                    pool.wait_ge(rowx_ready, b + 1)
                    pool.wait_ge(probs_ready, b + 1)
                    pool.wait_ge(slots_ready, b + 1)
                for k in range(TOPK):
                    pool.indirect_dma_start(
                        out=routed, out_offset=bass.IndirectOffsetOnAxis(ap=slots[:, t, k:k + 1], axis=0),
                        in_=rows[:, t, :], in_offset=None).then_inc(scatter_done, 16)
            pool.wait_ge(acc_init, 16 * (T // CAP + 1 + 2 + NB))

            with pool.Fori(0, NE // 4) as q:
                for k in range(4):
                    pool.wait_ge(oa_out, q * 4 + k + 1)
                    pool.wait_ge(ob_out, q * 4 + k + 1)
                    carry_wait(pool)
                    for j in range(CAPT):
                        pool.indirect_dma_start(
                            out=acc[k % 2], out_offset=bass.IndirectOffsetOnAxis(
                                ap=xt[k][:, j, IDC:IDC + 1].bitcast(i32), axis=0),
                            in_=osb[k % 2][:, j, :], in_offset=None, compute_op=ALU.add).then_inc(added[k % 2], 16)
            pool.wait_ge(ov_stored, 16)
            total = pool.value_load(over_table[0:1, 3:4], min_val=0, max_val=MAX_OVER)
            with pool.If(total > 0):
                with pool.Fori(0, total) as t:
                    pool.wait_ge(v_osb, t + 1)
                    carry_wait(pool)
                    pool.indirect_dma_start(
                        out=acc[0], out_offset=bass.IndirectOffsetOnAxis(
                            ap=xt[0][:, 0, IDC:IDC + 1].bitcast(i32), axis=0),
                        in_=osb[0][:, 0, :], in_offset=None, compute_op=ALU.add).then_inc(v_add, 16)

        @block.tensor
        def _(pe):
            pe.wait_ge(s_prep, 1)
            pe.wait_ge(s_w, 16 * 8)

            def transposes(dst, src, n_tok):
                for c in range(DC):
                    for t in range(n_tok):
                        last = pe.transpose(dst[:, (c * n_tok + t) * P:(c * n_tok + t + 1) * P],
                                            src[:, t, c * P:(c + 1) * P], ident)
                return last

            def xn_transposes(b):
                wait(pe, xn_ready, b + 1)
                transposes(ps_x0, xn, QT).then_inc(xnT_ps, 1)

            def project(dst, w, done):
                for m in range(DC):
                    for c in range(DC):
                        last = pe.matmul(dst[:, m * SEQ:(m + 1) * SEQ], w[:, c, m * P:(m + 1) * P], xnT[:, c, :],
                                         start=(c == 0), stop=(c == DC - 1))
                last.then_inc(done, 1)

            def token_major(dst, src, w, done):
                n = w.shape[2]
                for t in range(QT):
                    for c in range(DC):
                        last = pe.matmul(dst[:, t * n:(t + 1) * n], src[:, c, t * P:(t + 1) * P], w[:, c, :],
                                         start=(c == 0), stop=(c == DC - 1))
                last.then_inc(done, 1)

            def scores(b, par, s, u):
                m, r = s // 4, 32 * (s % 4)
                q, k = qT[par][r:r + 32, m, :], kT[par][r:r + 32, m, :, :]
                if s == 0:
                    wait(pe, q_ready, b + 1)
                    wait(pe, k_ready, b + 1)
                wait(pe, p1_ready, u)
                pe.matmul(ps_s1[:, :], q[:, P:SEQ], k, start=True, stop=False)
                pe.matmul(ps_s1[:, :].rearrange("p (h k) -> p h k", h=2)[:, :, P:SEQ], ident_b[:, :],
                          causal_b[:, :].unsqueeze(1).broadcast_to([P, 2, P]), start=False, stop=True).then_inc(s1_done, 1)
                wait(pe, p0_ready, u)
                pe.matmul(ps_s0[:, 0:2 * P], q[:, 0:P], k[:, :, 0:P], start=True, stop=False)
                pe.matmul(ps_s0[:, 0:2 * P].rearrange("p (h k) -> p h k", h=2), ident_b[:, :],
                          causal_b[:, :].unsqueeze(1).broadcast_to([P, 2, P]), start=False, stop=True).then_inc(s0_done, 1)

            def prob_transposes(s, u):
                wait(pe, p1_ready, u + 1)
                wait(pe, pt1_ready, u)
                for h in range(2):
                    for kt in range(QT):
                        last = pe.transpose(ps_t1[:, (h * QT + kt) * P:(h * QT + kt + 1) * P],
                                            pr1[s % 2][:, h, kt * P:(kt + 1) * P], ident)
                last.then_inc(t1_done, 1)
                wait(pe, p0_ready, u + 1)
                wait(pe, pt0_ready, u)
                for h in range(2):
                    last = pe.transpose(ps_t0[:, h * P:(h + 1) * P], pr0[s % 2][:, h, :], ident)
                last.then_inc(t0_done, 1)

            def values(b, par, s, u):
                if s == 0:
                    wait(pe, attn_ready, b)
                    wait(pe, v_ready, b + 1)
                wait(pe, pt1_ready, u + 1)
                wait(pe, pt0_ready, u + 1)
                for h in range(2):
                    head = 2 * s + h
                    col = slice(head * VW, (head + 1) * VW)
                    pe.matmul(ps_o0[:, col], pt0[s % 2][:, h, :], vt[par][:, 0, head, :], start=True, stop=True)
                    for kt in range(QT):
                        last = pe.matmul(ps_o1[:, col], pt1[s % 2][:, h * QT + kt, :], vt[par][:, kt, head, :],
                                         start=(kt == 0), stop=(kt == QT - 1))
                last.then_inc(av_done, 1)

            xn_transposes(0)
            wait(pe, xnT_ready, 1)
            project(ps_x1, wqs, q_ps)
            project(ps_x0, wks, k_ps)
            wait(pe, q_ready, 1)
            token_major(ps_x1, xnT, wvs, v_ps)
            wait(pe, k_ready, 1)

            def step(b, par, n):
                now, pre, post, old = n < NB, n < NB - 1, 1 <= n <= NB, n >= 2
                for s in range(PAIRS):
                    u = unit(b, s)
                    if now:
                        scores(b, par, s, u)
                    if (now and (n, s) != (0, 0)) or (n == NB and s == 0):
                        prob_transposes(s - 1, u - 1)
                    if s >= 2 and now:
                        values(b, par, s - 2, u - 2)
                    elif s < 2 and post:
                        values(b - 1, 1 - par, s + PAIRS - 2, u - 2)
                    if s == 0 and pre:
                        wait(pe, x2T_ready, b - 1 if n >= 2 else 0)
                        xn_transposes(b + 1)
                    if s == 0 and old:
                        wait(pe, x2T_ready, b - 1)
                        wait(pe, x2_ready, b - 1)
                        token_major(ps_x1, x2T, gates, lg_ps)
                    if s == 1 and pre:
                        wait(pe, xnT_ready, b + 2)
                        wait(pe, v_ready, b + 1)
                        if old:
                            wait(pe, lg_read, b - 1)
                        project(ps_x1, wqs, q_ps)
                    if s == 2 and pre:
                        project(ps_x0, wks, k_ps)
                    if s == 3 and pre:
                        wait(pe, q_ready, b + 2)
                        token_major(ps_x1, xnT, wvs, v_ps)
                    if s == 4 and post:
                        wait(pe, attn_ready, b)
                        if pre:
                            wait(pe, k_ready, b + 2)
                        transposes(ps_x0, attn, QT).then_inc(aT_ps, 1)
                    if s == 5 and post:
                        wait(pe, aT_ready, b)
                        if pre:
                            wait(pe, v_ready, b + 2)
                        if old:
                            wait(pe, lg_read, b - 1)
                        token_major(ps_x1, aT, wos, wo_ps)
                    if s == 6 and old:
                        wait(pe, mask_ready, b - 1)
                        if post:
                            wait(pe, aT_ready, b)
                        for t in range(QT):
                            dst = ps_x0[:, t * NE:(t + 1) * NE]
                            pe.matmul(dst, before_b[:, :], chosen[:, t, :], start=True, stop=False)
                            for j in range(t):
                                pe.matmul(dst, ones_b[:, :], chosen[:, j, :], start=False, stop=False)
                            last = pe.matmul(dst, ones_b[:, :], seen[:, :], start=False, stop=True)
                        last.then_inc(rank_ps, 1)
                    if s == 7 and post:
                        wait(pe, xn2_ready, b)
                        if old:
                            wait(pe, rank_read, b - 1)
                        transposes(ps_x0, xn2, QT).then_inc(x2T_ps, 1)

            batches(pe, step)
            pe.wait_ge(slots_ready, NB)
            pe.matmul(ps_x0[:, 0:NE], ones_b[:, :], seen[:, :], start=True, stop=True).then_inc(cnt_ps, 1)

            def x_transposes(src, tiles, done):
                for c in range(DC):
                    for j in range(tiles):
                        last = pe.transpose(ps_tx[c][:, j * P:(j + 1) * P], src[:, j, c * P:(c + 1) * P], ident)
                    last.then_inc(done[c], 1)

            def gate_up(w, src, n, g_done, u_done, u_free):
                for i, (dst, done) in enumerate(((ps_g, g_done), (ps_u, u_done))):
                    if i == 1:
                        u_free()
                    for c in range(DC):
                        at = c * 2 * INTER + i * INTER
                        last = pe.matmul(dst[:, 0:n], w[:, at:at + INTER], src[:, c, 0:n],
                                         start=(c == 0), stop=(c == DC - 1))
                    if done is not None:
                        last.then_inc(done, 1)

            def down(w, h, k, j):
                dst = ps_oa[k][:, j * D:(j + 1) * D] if j < 2 else ps_ob[k][:, 0:D]
                return pe.matmul(dst, h[:, j * P:(j + 1) * P], w[:, DC * 2 * INTER:WW], start=True, stop=True)

            def turn(q, k):
                pe.wait_ge(xt_in[k], (q + 1) * 16)
                for c in range(DC):
                    wait(pe, xT_ready[c], q * 4 + k)
                x_transposes(xt[k], CAPT, tx_ps)

            pe.wait_ge(ov_ready, 1)
            turn(0, 0)

            def expert(q, k, n):
                e = q * 4 + k
                if n < NE - 1:
                    turn(*after(q, k))
                if n < NE:
                    pe.wait_ge(w_in[k], (q + 1) * 16)
                    for c in range(DC):
                        pe.wait_ge(xT_ready[c], e + 1)
                    wait(pe, sg_ready, e)
                    gate_up(wexp[k], xT[k % 2], CAP, g_ps, u_ps, lambda: wait(pe, h_ready, e))
                if n > 0:
                    wait(pe, h_ready, e)
                    wait(pe, oa_out, e - 2)
                    wait(pe, ob_out, e - 2)
                    kk = (k - 1) % 4
                    for j in range(CAPT):
                        o = down(wexp[kk], hT[kk % 2], kk % 2, j)
                        if j == 1:
                            o.then_inc(oa_ps, 1)
                    o.then_inc(ob_ps, 1)

            expert_loop(pe, expert)
            pe.wait_ge(ov_stored, 16)
            total = pe.value_load(over_table[0:1, 3:4], min_val=0, max_val=MAX_OVER)
            with pe.If(total > 0):
                with pe.Fori(0, total) as t:
                    pe.wait_ge(v_ld, t * 32 + 32)
                    for c in range(DC):
                        o = pe.transpose(ps_tx[c][:, 0:P], xt[0][:, 0, c * P:(c + 1) * P], ident)
                    o.then_inc(v_tx, 1)
                    pe.wait_ge(v_xT, t + 1)
                    gate_up(wexp[0], xT[0], P, None, v_gu, lambda: None)
                    pe.wait_ge(v_h, t + 1)
                    down(wexp[0], hT[0], 0, 0).then_inc(v_o, 1)

        @block.scalar
        def _(act):
            act.wait_ge(s_w, 16 * 8)
            act.wait_ge(s_cst, 32)
            for h, mask in enumerate((C_EVEN, C_ODD)):
                last = act.activation(bkm[:, h, :], bqks[:, DC:2 * DC], ACT.Copy, scale=cst[:, mask:mask + 1])
            last.then_inc(s_bkm, 1)
            act.wait_ge(s_bkm, 1)

            def copy(dst, src, ready, done, value):
                wait(act, ready, value)
                act.copy(dst, src).then_inc(done, 1)

            def flat(a):
                return a[:, :, :].rearrange("p a b -> p (a b)")

            def q_out(b, par):
                wait(act, q_ps, b + 1)
                for m in range(DC):
                    last = act.activation(qT[par][:, m, :], ps_x1[:, m * SEQ:(m + 1) * SEQ], ACT.Identity,
                                          bias=bqks[:, m:m + 1], scale=1.0)
                last.then_inc(q_ready, 1)

            def k_out(b, par):
                wait(act, k_ps, b + 1)
                for m in range(DC):
                    for h, mask in enumerate((C_EVEN, C_ODD)):
                        last = act.activation(kT[par][:, m, h, :], ps_x0[:, m * SEQ:(m + 1) * SEQ], ACT.Identity,
                                              bias=bkm[:, h, m:m + 1], scale=cst[:, mask:mask + 1])
                last.then_inc(k_ready, 1)

            copy(flat(xnT), ps_x0[:, :], xnT_ps, xnT_ready, 1)
            q_out(0, 0)
            k_out(0, 0)

            def step(b, par, n):
                now, pre, post, old = n < NB, n < NB - 1, 1 <= n <= NB, n >= 2
                for s in range(PAIRS):
                    u = unit(b, s)
                    if now:
                        wait(act, nm1_ready, u + 1)
                        wait(act, t0_done, u - 1)
                        for h in range(2):
                            last = act.activation(pr1[s % 2][:, h, :], ps_s1[:, h * SEQ:(h + 1) * SEQ], ACT.Exp,
                                                  bias=nm[:, s % 2, h:h + 1], scale=SCALE)
                        last.then_inc(p1_ready, 1)
                        wait(act, nm0_ready, u + 1)
                        for h in range(2):
                            last = act.activation(pr0[s % 2][:, h, :], ps_s0[:, h * P:(h + 1) * P], ACT.Exp,
                                                  bias=nm[:, s % 2, 2 + h:3 + h], scale=SCALE)
                        last.then_inc(p0_ready, 1)
                    if (now and (n, s) != (0, 0)) or (n == NB and s == 0):
                        wait(act, t0_done, u)
                        wait(act, av_done, u - 2)
                        act.copy(flat(pt0[(s - 1) % 2]), ps_t0[:, 0:2 * P]).then_inc(pt0_ready, 1)
                    if s == 0 and pre:
                        copy(flat(xnT), ps_x0[:, :], xnT_ps, xnT_ready, b + 2)
                    if s == 1 and pre:
                        q_out(b + 1, 1 - par)
                    if s == 2 and pre:
                        k_out(b + 1, 1 - par)
                    if s == 3 and old:
                        wait(act, mask_ready, b - 1)
                        for t in range(QT):
                            last = act.activation(elg[:, t, :], lg[:, t, :], ACT.Exp, bias=nmx[:, t:t + 1], scale=1.0,
                                                  accum_out=esum[:, t:t + 1])
                        last.then_inc(e_ready, 1)
                    if s == 4 and post:
                        copy(flat(aT), ps_x0[:, :], aT_ps, aT_ready, b)
                    if s == 6 and post:
                        wait(act, xn2_ready, b)
                        act.copy(rows[:, bass.ds((b - 1) * QT, QT), 0:D], xn2[:, :, :]).then_inc(rowx_ready, 1)
                    if s == 7 and post:
                        copy(flat(x2T), ps_x0[:, :], x2T_ps, x2T_ready, b)

            batches(act, step)

            def x_out(q, k):
                act.wait_ge(tx_ps[0], q * 4 + k + 1)
                act.copy(xT[k % 2][:, 0, :], ps_tx[0][:, 0:CAP]).then_inc(xT_ready[0], 1)

            x_out(0, 0)

            def expert(q, k, n):
                e = q * 4 + k
                if n < NE - 1:
                    x_out(*after(q, k))
                if n < NE:
                    act.wait_ge(g_ps, e + 1)
                    act.activation(sg[k % 2][:, :], ps_g[:, 0:CAP], ACT.Silu).then_inc(sg_ready, 1)
                if n > 0:
                    kk = (k - 1) % 4
                    act.wait_ge(oa_ps, e)
                    wait(act, added[kk % 2], earlier_adds(*before(q, k)))
                    for j in range(2):
                        last = act.activation(osb[kk % 2][:, j, :], ps_oa[kk % 2][:, j * D:(j + 1) * D], ACT.Copy,
                                              scale=xt[kk][:, j, bass.ds(e - 1 + PRC, 1)])
                    last.then_inc(oa_out, 1)

            expert_loop(act, expert)
            act.wait_ge(ov_stored, 16)
            total = act.value_load(over_table[0:1, 3:4], min_val=0, max_val=MAX_OVER)
            with act.If(total > 0):
                with act.Fori(0, total) as t:
                    act.wait_ge(v_gu, t + 1)
                    act.activation(sg[0][:, 0:P], ps_g[:, 0:P], ACT.Silu).then_inc(v_sg, 1)

        @block.vector
        def _(dve):
            dve.wait_ge(s_cst, 32)
            for dst, at in ((ident_b, C_ID), (before_b, C_LT), (causal_b, C_CAUSAL)):
                dve.tensor_copy(dst[:, :], cst[:, at:at + P])
            dve.memset(pad_rows[:, :, :].rearrange("p a b -> p (a b)"), 0.0).then_inc(pad_link, 1)
            for t in vt:
                dve.memset(t[:, :, :, :].rearrange("p a b c -> p (a b c)"), 1.0)
            dve.memset(ones_b[:, :], 1.0)
            dve.memset(onese[:, :], 1.0)
            dve.memset(seen[:, :], 0.0).then_inc(s_prep, 1)
            dve.tensor_copy(rows[:, :, IDC].bitcast(i32), idt[:, CAPT:CAPT + NT])
            dve.wait_ge(pad_link, 1)
            dve.tensor_copy(pad_rows[:, :, IDC].bitcast(i32), idt[:, 0:CAPT]).then_inc(s_padrow, 1)
            dve.wait_ge(s_prep, 1)
            dve.wait_ge(s_w, 16 * 8)

            def norm(i, n, src, dst, done):
                g, link, at = ln[i], ln_link[i], [n * LN_LINKS]

                def linked(ins):
                    ins.then_inc(link, 1)
                    at[0] = at[0] + 1
                    dve.wait_ge(link, at[0])

                carry_wait(dve)
                for t in range(QT):
                    last = dve.bn_stats(g["stats"][:, t, :], src(t))
                linked(last)
                carry_wait(dve)
                for t in range(QT):
                    last = dve.bn_aggr(g["mv"][:, t, :], g["stats"][:, t, :])
                linked(last)
                var = g["mv"][:, :, 1]
                dve.tensor_scalar(g["half"][:, :], var, EPS, -0.5, ALU.add, ALU.mult)
                linked(dve.tensor_scalar(g["ve"][:, :], var, EPS, None, ALU.add))
                linked(dve.tensor_scalar(g["sh"][:, :], g["ve"][:, :].bitcast(i32), 1, None, ALU.arith_shift_right))
                linked(dve.tensor_scalar(g["r"][:, :].bitcast(i32), g["sh"][:, :], -1.0, float(RSQRT_MAGIC),
                                         ALU.mult, ALU.add))
                for _ in range(NEWTON):
                    linked(dve.tensor_tensor(g["t"][:, :], g["r"][:, :], g["r"][:, :], ALU.mult))
                    linked(dve.tensor_tensor(g["t"][:, :], g["t"][:, :], g["half"][:, :], ALU.mult))
                    linked(dve.scalar_tensor_tensor(g["r"][:, :], g["t"][:, :], 1.5, g["r"][:, :], ALU.add, ALU.mult))
                for t in range(QT):
                    last = dve.tensor_scalar(dst[:, t, :], src(t), g["mv"][:, t, 0:1], g["r"][:, t:t + 1],
                                             ALU.subtract, ALU.mult)
                last.then_inc(done, 1)

            def norm1(b):
                norm(0, b, lambda t: xall[:, b * QT + t, :], xn, xn_ready)

            def v_out(b, par):
                wait(dve, v_ps, b + 1)
                for t in range(QT):
                    last = dve.tensor_tensor(
                        vt[par][:, t, :, 0:HD], ps_x1[:, t * D:(t + 1) * D].rearrange("p (h d) -> p h d", d=HD),
                        bvs[:, :].rearrange("p (h d) -> p h d", d=HD), ALU.add)
                last.then_inc(v_ready, 1)

            dve.wait_ge(s_x0, 16)
            norm1(0)
            dve.wait_ge(xnT_ps, 1)
            dve.wait_ge(s_xrest, 16)
            norm1(1)
            v_out(0, 0)

            def step(b, par, n):
                now, pre, post, old = n < NB, n < NB - 1, 1 <= n <= NB, n >= 2
                for s in range(PAIRS):
                    u, sp_ = unit(b, s), s % 2
                    if now:
                        wait(dve, s1_done, u + 1)
                        dve.reduce_max(mx[:, sp_, 0:2], ps_s1[:, :].rearrange("p (h k) -> p h k", h=2),
                                       axis=AX.X).then_inc(mx_link, 1)
                        wait(dve, s0_done, u + 1)
                        dve.reduce_max(mx[:, sp_, 2:4], ps_s0[:, 0:2 * P].rearrange("p (h k) -> p h k", h=2),
                                       axis=AX.X).then_inc(mx_link, 1)
                        for i, done in enumerate((nm1_ready, nm0_ready)):
                            wait(dve, mx_link, u * 2 + 1 + i)
                            dve.tensor_scalar(nm[:, sp_, 2 * i:2 * i + 2], mx[:, sp_, 2 * i:2 * i + 2], -SCALE, None,
                                              ALU.mult).then_inc(done, 1)
                    if (now and (n, s) != (0, 0)) or (n == NB and s == 0):
                        wait(dve, t1_done, u)
                        wait(dve, av_done, u - 2)
                        dve.tensor_copy(pt1[(s - 1) % 2][:, :, :].rearrange("p a b -> p (a b)"), ps_t1[:, :])\
                            .then_inc(pt1_ready, 1)
                    if s == 0 and old:
                        wait(dve, lg_ps, b - 1)
                        dve.tensor_copy(lg[:, :, :].rearrange("p a b -> p (a b)"), ps_x1[:, 0:QT * NE]).then_inc(lg_read, 1)
                        wait(dve, lg_read, b - 1)
                        carry_wait(dve)
                        for t in range(QT):
                            last = dve.max(top[:, t, :], lg[:, t, :])
                        last.then_inc(top_link, 1)
                        wait(dve, top_link, b * 2 - 3)
                        dve.tensor_scalar(nmx[:, :], top[:, :, 0], -1.0, None, ALU.mult)
                        for t in range(QT):
                            last = dve.match_replace(rest[:, t, :], top[:, t, :], lg[:, t, :], -3e38)
                        last.then_inc(top_link, 1)
                        wait(dve, top_link, b * 2 - 2)
                        dve.tensor_tensor(chosen[:, :, :], rest[:, :, :], lg[:, :, :], ALU.is_lt).then_inc(mask_ready, 1)
                    if s == 1 and post:
                        wait(dve, av_done, b * PAIRS)
                        for t, o in enumerate((ps_o0, ps_o1)):
                            last = dve.reciprocal(rden[:, t, :], o[:, 0:NH * VW].rearrange("p (h v) -> p h v", v=VW)[:, :, HD])
                        last.then_inc(norm_link, 1)
                        wait(dve, norm_link, b)
                        for t, o in enumerate((ps_o0, ps_o1)):
                            last = dve.tensor_tensor(
                                attn[:, t, :].rearrange("p (h d) -> p h d", d=HD),
                                o[:, 0:NH * VW].rearrange("p (h v) -> p h v", v=VW)[:, :, 0:HD],
                                rden[:, t, :].unsqueeze(2).broadcast_to([P, NH, HD]), ALU.mult)
                        last.then_inc(attn_ready, 1)
                    if s == 3 and pre:
                        v_out(b + 1, 1 - par)
                    if s == 4 and old:
                        wait(dve, e_ready, b - 1)
                        dve.reciprocal(erec[:, :], esum[:, :]).then_inc(pr_link, 1)
                        wait(dve, pr_link, b - 1)
                        for t in range(QT):
                            last = dve.tensor_scalar(rows[:, (b - 2) * QT + t, PRC:RW], elg[:, t, :], erec[:, t:t + 1],
                                                     None, ALU.mult)
                        last.then_inc(probs_ready, 1)
                    if s == 5 and post:
                        wait(dve, wo_ps, b)
                        mine = xall[:, bass.ds((b - 1) * QT, QT), :]
                        dve.tensor_tensor(mine, ps_x1[:, :].rearrange("p (t d) -> p t d", d=D), mine, ALU.add)\
                            .then_inc(x2_link, 1)
                        wait(dve, x2_link, b)
                        dve.tensor_tensor(mine, mine, bos[:, :].unsqueeze(1).broadcast_to([P, QT, D]), ALU.add)\
                            .then_inc(x2_ready, 1)
                        wait(dve, x2_ready, b)
                        if old:
                            wait(dve, x2T_ps, b - 1)
                            wait(dve, rowx_ready, b - 1)
                        norm(1, b - 1, lambda t: xall[:, (b - 1) * QT + t, :], xn2, xn2_ready)
                    if s == 6 and old:
                        wait(dve, rank_ps, b - 1)
                        dve.tensor_tensor(place[:, :, :], ps_x0[:, 0:QT * NE].rearrange("p (t e) -> p t e", e=NE),
                                          cst[:, C_BASE:C_BASE + NE].unsqueeze(1).broadcast_to([P, QT, NE]),
                                          ALU.add).then_inc(rank_read, 1)
                        dve.tensor_tensor(seen[:, :], seen[:, :], chosen[:, 0, :], ALU.add).then_inc(sl_link, 1)
                        wait(dve, rank_read, b - 1)
                        dve.tensor_tensor(place[:, :, :], place[:, :, :], chosen[:, :, :], ALU.mult).then_inc(sl_link, 1)
                        wait(dve, sl_link, b * 3 - 5)
                        dve.tensor_tensor(seen[:, :], seen[:, :], chosen[:, 1, :], ALU.add)
                        wait(dve, sl_link, b * 3 - 4)
                        carry_wait(dve)
                        for t in range(QT):
                            last = dve.max(slotf[:, t, :], place[:, t, :])
                        last.then_inc(sl_link, 1)
                        wait(dve, sl_link, b * 3 - 3)
                        dve.tensor_scalar(slots[:, bass.ds((b - 2) * QT, QT), :], slotf[:, :, :], -1.0, None,
                                          ALU.add).then_inc(slots_ready, 1)
                    if s == 7 and n < NB - 2:
                        wait(dve, xnT_ps, b + 2)
                        norm1(b + 2)

            batches(dve, step)

            links = [0]

            def linked(ins):
                ins.then_inc(ov_link, 1)
                links[0] += 1
                dve.wait_ge(ov_link, links[0])

            dve.wait_ge(cnt_ps, 1)
            linked(dve.tensor_copy(cnt[:, :], ps_x0[:, 0:NE]))
            linked(dve.tensor_tensor(gt[:, :, :], cnt[:, :].unsqueeze(2).broadcast_to([P, NE, OVT]),
                                     cst[:, C_THR:C_THR + OVT].unsqueeze(1).broadcast_to([P, NE, OVT]), ALU.is_gt))
            linked(dve.reduce_sum(nov[:, :], gt[:, :, :], axis=AX.X))
            linked(dve.tensor_tensor_scan(cum[:, :], onese[:, :], nov[:, :], 0.0, ALU.mult, ALU.add))
            linked(dve.tensor_scalar(ge[:, :], cum[:, :], cst[:, C_IOTA:C_IOTA + 1], None, ALU.is_le))
            dve.reduce_sum(ovv[:, 1:2], ge[:, :], axis=AX.X)
            linked(dve.tensor_tensor(ge[:, :], ge[:, :], nov[:, :], ALU.mult))
            linked(dve.reduce_sum(ovv[:, 4:5], ge[:, :], axis=AX.X))
            linked(dve.tensor_scalar(eq[:, :], cst[:, C_EIDX:C_EIDX + NE], ovv[:, 1:2], None, ALU.is_equal))
            linked(dve.tensor_tensor(eq[:, :], eq[:, :], cnt[:, :], ALU.mult))
            linked(dve.reduce_sum(ovv[:, 5:6], eq[:, :], axis=AX.X))
            linked(dve.tensor_tensor(ovv[:, 6:7], cst[:, C_IOTA:C_IOTA + 1], ovv[:, 4:5], ALU.subtract))
            linked(dve.tensor_scalar(ovv[:, 6:7], ovv[:, 6:7], float(P), float(CAP), ALU.mult, ALU.add))
            linked(dve.scalar_tensor_tensor(ovv[:, 0:1], ovv[:, 1:2], float(REG), ovv[:, 6:7], ALU.mult, ALU.add))
            linked(dve.scalar_tensor_tensor(ovv[:, 2:3], ovv[:, 1:2], float(REG), ovv[:, 5:6], ALU.mult, ALU.add))
            linked(dve.tensor_copy(ovv[:, 3:4], cum[:, NE - 1:NE]))
            dve.tensor_copy(ovi[:, :], ovv[:, 0:4]).then_inc(ov_ready, 1)

            def x_out(q, k):
                dve.wait_ge(tx_ps[1], q * 4 + k + 1)
                dve.tensor_copy(xT[k % 2][:, 1, :], ps_tx[1][:, 0:CAP]).then_inc(xT_ready[1], 1)

            x_out(0, 0)

            def expert(q, k, n):
                e = q * 4 + k
                if n < NE - 1:
                    x_out(*after(q, k))
                if n < NE:
                    dve.wait_ge(sg_ready, e + 1)
                    dve.wait_ge(u_ps, e + 1)
                    dve.tensor_tensor(hT[k % 2][:, :], sg[k % 2][:, :], ps_u[:, 0:CAP], ALU.mult).then_inc(h_ready, 1)
                if n > 0:
                    kk = (k - 1) % 4
                    dve.wait_ge(ob_ps, e)
                    wait(dve, added[kk % 2], earlier_adds(*before(q, k)))
                    dve.tensor_scalar(osb[kk % 2][:, 2, :], ps_ob[kk % 2][:, 0:D],
                                      xt[kk][:, 2, bass.ds(e - 1 + PRC, 1)], None, ALU.mult).then_inc(ob_out, 1)

            expert_loop(dve, expert)

            dve.wait_ge(ov_stored, 16)
            total = dve.value_load(over_table[0:1, 3:4], min_val=0, max_val=MAX_OVER)
            with dve.If(total > 0):
                with dve.Fori(0, total) as t:
                    e = dve.value_load(over_table[bass.ds(t, 1), 1:2], min_val=0, max_val=NE - 1)
                    dve.wait_ge(v_tx, t + 1)
                    for c in range(DC):
                        last = dve.tensor_copy(xT[0][:, c, 0:P], ps_tx[c][:, 0:P])
                    last.then_inc(v_xT, 1)
                    dve.wait_ge(v_sg, t + 1)
                    dve.tensor_tensor(hT[0][:, 0:P], sg[0][:, 0:P], ps_u[:, 0:P], ALU.mult).then_inc(v_h, 1)
                    dve.wait_ge(v_o, t + 1)
                    dve.tensor_scalar(osb[0][:, 0, :], ps_oa[0][:, 0:D], xt[0][:, 0, bass.ds(e + PRC, 1)], None,
                                      ALU.mult).then_inc(v_osb, 1)

            for c in range(4):
                n = NT // 4
                mine = xall[:, n * c:n * c + n, :]
                dve.wait_ge(f_in[c], 32)
                dve.tensor_tensor(mine, mine, rows[:, n * c:n * c + n, 0:D], ALU.add).then_inc(f_sum, 1)


def kernel(**inputs):
    import concourse.bacc as bacc
    from concourse import mybir as mb
    from concourse.bass_utils import run_bass_kernel_spmd

    a = {k: np.asarray(v) for k, v in inputs.items()}
    w13, w2 = a["L0_ffn_w13"], a["L0_ffn_w2"]
    w13t = np.transpose(w13.reshape(NE, 2 * INTER, DC, P), (0, 3, 2, 1)).reshape(NE, P, DC * 2 * INTER)
    experts = np.concatenate([w13t, np.transpose(w2, (0, 2, 1))], axis=2)
    bq, bk = a["L0_attn_bq"].reshape(DC, P), a["L0_attn_bk"].reshape(DC, P)
    p = np.arange(P)
    consts = np.zeros((P, C_END), np.float32)
    consts[:, C_ID:C_ID + P] = np.eye(P)
    consts[:, C_LT:C_LT + P] = p[:, None] < p[None, :]
    consts[:, C_CAUSAL:C_CAUSAL + P] = np.where(p[None, :] > p[:, None], LOW, 0.0)
    consts[:, C_BASE:C_BASE + NE] = np.arange(NE) * REG + 1
    consts[:, C_EVEN] = p % 32 < HD
    consts[:, C_ODD] = p % 32 >= HD
    consts[:, C_EIDX:C_EIDX + NE] = np.arange(NE)
    consts[:, C_IOTA] = p
    consts[:, C_THR:C_THR + OVT] = CAP + P * np.arange(OVT)
    ids = np.concatenate([T + p[:, None] + P * np.arange(CAPT), p[:, None] + P * np.arange(NT)], axis=1)
    arrays = {
        "x": a["L0_attn_x"].reshape(T, D),
        "wq": a["L0_attn_wq"].T, "wk": a["L0_attn_wk"].T, "wv": a["L0_attn_wv"].T, "wo": a["L0_attn_wo"].T,
        "bqk": np.stack([*bq, *bk], axis=1), "bv": a["L0_attn_bv"][None, :], "bo": a["L0_attn_bo"][None, :],
        "gate": a["L0_ffn_gate_w"].T, "experts": experts, "consts": consts, "ids": ids.astype(np.int32),
    }
    arrays = {k: np.ascontiguousarray(v) for k, v in arrays.items()}
    nc = bacc.Bacc("TRN2", target_bir_lowering=False, num_devices=1)
    args = {k: nc.dram_tensor(k + "_dram", v.shape, mb.dt.from_np(v.dtype), kind="ExternalInput").ap()
            for k, v in arrays.items()}
    args["y"] = nc.dram_tensor("y_dram", (T, D), mb.dt.float32, kind="ExternalOutput").ap()
    program(nc, **args)
    r = run_bass_kernel_spmd(nc, [{k + "_dram": v for k, v in arrays.items()}], core_ids=[0])
    return r.results[0]["y_dram"].reshape(NB, SEQ, D)
```

```python
import numpy as np
import concourse.bass as bass
from concourse import mybir
from contextlib import ExitStack

NB, SEQ, D = 8, 256, 256
NH, HD = 16, 16
NE, TOPK, INTER = 64, 8, 128
P = 128
T = NB * SEQ
NT = T // P
QT = SEQ // P
DC = D // P
PAIRS = NH // 2
VW = HD + 1
CAPT = 3
CAP = CAPT * P
REG = T + P
IDC, PRC = D, D + 1
RW = D + 1 + NE
DUMMY = CAP
WW = DC * 2 * INTER + D
EPS = 1e-5
SCALE = float(HD) ** -0.5
LOW = -1e30
RSQRT_MAGIC = 0x5F3759DF
LN_CUT = 6
LN_LINKS = LN_CUT + 2 * 3
OVT = (T - CAP) // P
MAX_OVER = 112
LOOP_B = (2, 6)
C_ID, C_LT, C_CAUSAL, C_BASE, C_EVEN, C_ODD, C_EIDX, C_IOTA, C_THR, C_END = (
    np.cumsum([0, P, P, P, NE, 1, 1, NE, 1, OVT]).tolist())


def program(nc, x, wq, wk, wv, wo, bqk, bv, bo, gate, experts, consts, ids, y):
    fp32, bf16, i32 = mybir.dt.float32, mybir.dt.bfloat16, mybir.dt.int32
    ALU, ACT, AX = mybir.AluOpType, mybir.ActivationFunctionType, mybir.AxisListType

    routed = nc.dram_tensor("routed", [NE * REG, RW], fp32, kind="Internal").ap()
    acc = [nc.dram_tensor(f"acc{i}", [T + DUMMY, D], fp32, kind="Internal").ap() for i in range(2)]
    over_table = nc.dram_tensor("over_table", [P, 4], i32, kind="Internal").ap()

    ctx = ExitStack()
    with ctx:
        def sb(name, shape, dt=fp32):
            return ctx.enter_context(nc.sbuf_tensor(name, shape, dt))

        def sem(name):
            return ctx.enter_context(nc.semaphore(name))

        bank = [ctx.enter_context(nc.psum_tensor(f"bank{i}", [P, 512], fp32)) for i in range(8)]
        ps_s1, ps_s0, ps_t1, ps_t0, ps_o0, ps_o1, ps_x0, ps_x1 = bank
        ps_tx, ps_g, ps_u, ps_oa, ps_ob = (bank[0], bank[1]), bank[2], bank[3], (bank[4], bank[6]), (bank[5], bank[7])

        cst = sb("cst", [P, C_END])
        idt = sb("idt", [P, CAPT + NT], i32)
        ident = cst[:, C_ID:C_ID + P]
        ident_b = sb("ident_b", [P, P], bf16)
        before_b = sb("before_b", [P, P], bf16)
        causal_b = sb("causal_b", [P, P], bf16)
        ones_b = sb("ones_b", [P, P], bf16)
        wqs, wks, wvs, wos = (sb(n, [P, DC, D]) for n in ("wqs", "wks", "wvs", "wos"))
        gates = sb("gates", [P, DC, NE])
        bqks = sb("bqks", [P, 2 * DC])
        bqs = sb("bqs", [P, DC])
        bkm = sb("bkm", [P, 2, DC])
        bvs = sb("bvs", [P, DC])
        bvw = sb("bvw", [P, DC, P])
        bos = sb("bos", [P, D])
        pad_rows = sb("pad_rows", [P, CAPT, RW])
        xall = sb("xall", [P, NT, D])
        xn = sb("xn", [P, QT, D])
        xnT = sb("xnT", [P, DC, SEQ])
        qT = [sb(f"qT{i}", [P, DC, SEQ]) for i in range(2)]
        kT = [sb(f"kT{i}", [P, DC, 2, SEQ]) for i in range(2)]
        vt = [sb(f"vt{i}", [P, QT, NH, VW]) for i in range(2)]
        nm = sb("nm", [P, 2, 4])
        pr1 = [sb(f"pr1_{i}", [P, 2, SEQ]) for i in range(2)]
        pr0 = [sb(f"pr0_{i}", [P, 2, P]) for i in range(2)]
        pt1 = [sb(f"pt1_{i}", [P, 3, P]) for i in range(2)]
        pt0 = [sb(f"pt0_{i}", [P, 3, P]) for i in range(2)]
        rden = sb("rden", [P, QT, NH])
        attn = sb("attn", [P, QT, D])
        aT = sb("aT", [P, DC, SEQ])
        xn2 = sb("xn2", [P, QT, D])
        x2T = sb("x2T", [P, DC, SEQ])
        xb = sb("xb", [P, NT, D])
        st6 = sb("st6", [P, 2 * QT, 6])
        mv = sb("mv", [P, 2 * QT, 2])
        ve, hv, rs, tn = (sb(n, [P, 2 * QT]) for n in ("ve", "hv", "rs", "tn"))
        rows = sb("rows", [P, NT, RW])
        lg = sb("lg", [P, QT, NE])
        top = sb("top", [P, QT, TOPK])
        rest = sb("rest", [P, QT, NE])
        chosen = sb("chosen", [P, QT, NE], bf16)
        seen = sb("seen", [P, NE], bf16)
        nmx = sb("nmx", [P, QT])
        elg = sb("elg", [P, QT, NE])
        esum = sb("esum", [P, QT])
        erec = sb("erec", [P, QT])
        place = sb("place", [P, QT, NE])
        slotf = sb("slotf", [P, QT, TOPK])
        slots = sb("slots", [P, NT, TOPK], i32)
        cnt = sb("cnt", [P, NE])
        gt = sb("gt", [P, NE, OVT])
        nov = sb("nov", [P, NE])
        onese = sb("onese", [P, NE])
        cum = sb("cum", [P, NE])
        ge = sb("ge", [P, NE])
        eq = sb("eq", [P, NE])
        ovv = sb("ovv", [P, 8])
        ovi = sb("ovi", [P, 4], i32)
        wexp = [sb(f"wexp{i}", [P, WW]) for i in range(4)]
        xt = [sb(f"xt{i}", [P, CAPT, RW]) for i in range(4)]
        xT = [sb(f"xT{i}", [P, DC, CAP]) for i in range(2)]
        sg = [sb(f"sg{i}", [P, CAP]) for i in range(2)]
        hT = [sb(f"hT{i}", [P, CAP]) for i in range(2)]
        osb = [sb(f"osb{i}", [P, CAPT, D]) for i in range(2)]
        tok = [sb(f"tok{i}", [P, CAPT], i32) for i in range(4)]
        wgt = [sb(f"wgt{i}", [P, CAPT]) for i in range(4)]

        s_x0, s_xrest, s_w, s_cst = sem("x_first"), sem("x_rest"), sem("weights_in"), sem("consts_in")
        pad_link, s_held = sem("pad_link"), sem("wait_held")
        s_prep, s_padrow, s_bkm = sem("consts_ready"), sem("pad_row_ready"), sem("key_bias_ready")
        xn_ready, xnT_ps, xnT_ready = sem("xn_ready"), sem("xnT_ps"), sem("xnT_ready")
        q_ps, k_ps, v_ps = sem("q_ps"), sem("k_ps"), sem("v_ps")
        q_ready, k_ready, v_ready = sem("q_ready"), sem("k_ready"), sem("v_ready")
        s1_done, s0_done = sem("s1_done"), sem("s0_done")
        nm1_ready, nm0_ready = sem("nm1_ready"), sem("nm0_ready")
        p1_ready, p0_ready = sem("p1_ready"), sem("p0_ready")
        t1_done, t0_done = sem("t1_done"), sem("t0_done")
        pt1_ready, pt0_ready, av_done = sem("pt1_ready"), sem("pt0_ready"), sem("av_done")
        norm_link, attn_ready, aT_ps, aT_ready = sem("norm_link"), sem("attn_ready"), sem("aT_ps"), sem("aT_ready")
        wo_ps, x2_ready, xb_ready = sem("wo_ps"), sem("x2_ready"), sem("xb_ready")
        bvw_ready, bias_ps, bias_ready = sem("bvw_ready"), sem("bias_ps"), sem("bias_ready")
        ln_link, st_done = sem("ln_link"), [sem("st1_done"), sem("st2_done")]
        xn2_ready, x2T_ps, x2T_ready = sem("xn2_ready"), sem("x2T_ps"), sem("x2T_ready")
        lg_ps, lg_read, top_link, mask_ready = sem("lg_ps"), sem("lg_read"), sem("top_link"), sem("mask_ready")
        e_ready, pr_link, probs_ready, rowx_ready = sem("e_ready"), sem("pr_link"), sem("probs_ready"), sem("rowx_ready")
        rank_ps, rank_read, sl_link, slots_ready = sem("rank_ps"), sem("rank_read"), sem("sl_link"), sem("slots_ready")
        prefill_done, acc_init = sem("prefill_done"), sem("acc_init")
        scattered = [sem(f"scattered{k}") for k in range(TOPK)]
        cnt_ps, ov_link, ov_ready, ov_stored = sem("cnt_ps"), sem("ov_link"), sem("ov_ready"), sem("ov_stored")
        w_in = [sem(f"w_in{i}") for i in range(4)]
        xt_in = [sem(f"xt_in{i}") for i in range(4)]
        tx_ps = [sem("tx0_ps"), sem("tx1_ps")]
        xT_ready = [sem("xT0_ready"), sem("xT1_ready")]
        g_ps, u_ps, sg_ready, h_ready = sem("g_ps"), sem("u_ps"), sem("sg_ready"), sem("h_ready")
        oa_ps, ob_ps, oa_out, ob_out = sem("oa_ps"), sem("ob_ps"), sem("oa_out"), sem("ob_out")
        added, tw_ready = [sem("added0"), sem("added1")], sem("tw_ready")
        v_pad, v_ld, v_tx, v_xT, v_gu, v_sg, v_h = (sem("v_" + n) for n in ("pad", "ld", "tx", "xT", "gu", "sg", "h"))
        v_o, v_osb, v_add = sem("v_o"), sem("v_osb"), sem("v_add")
        f_in, f_sum, f_out = [sem(f"f_in{i}") for i in range(4)], sem("f_sum"), sem("f_out")

        block = ctx.enter_context(nc.Block())

        def wait(eng, s, value):
            if not isinstance(value, int) or value > 0:
                eng.wait_ge(s, value)

        def carry_wait(eng):
            eng.sem_inc(s_held, 1)

        def batches(eng, step):
            lo, hi = LOOP_B
            for b in range(lo):
                step(b, b % 2, b)
            with eng.Fori(0, (hi - lo) // 2) as i:
                step(i * 2 + lo, 0, lo)
                step(i * 2 + lo + 1, 1, lo)
            for b in range(hi, NB + 2):
                step(b, b % 2, b)

        def expert_loop(eng, step):
            for k in range(4):
                step(0, k, k)
            with eng.Fori(1, NE // 4 - 1) as q:
                for k in range(4):
                    step(q, k, 4 + k)
            for e in range(NE - 4, NE + 1):
                step(e // 4, e % 4, e)

        def before(q, k):
            return (q, k - 1) if k else (q - 1, 3)

        def after(q, k):
            return (q, k + 1) if k < 3 else (q + 1, 0)

        def earlier_adds(q, k):
            return (q * 2 + k // 2) * (16 * CAPT)

        def unit(b, s):
            return b * PAIRS + s

        @block.sync
        def _(sp):
            sp.dma_start(xall[:, 0:QT, :], x[0:SEQ, :].rearrange("(t p) d -> p t d", p=P)).then_inc(s_x0, 16)
            sp.dma_start(cst[:, :], consts).then_inc(s_cst, 16)
            sp.dma_start(idt[:, :], ids).then_inc(s_cst, 16)
            for dst, src in ((wqs, wq), (wks, wk), (wvs, wv), (wos, wo), (gates, gate)):
                sp.dma_start(dst[:, :, :], src.rearrange("(c p) o -> p c o", p=P)).then_inc(s_w, 16)
            sp.dma_start(bqks[:, :], bqk).then_inc(s_w, 16)
            sp.dma_start(bvs[:, :], bv).then_inc(s_w, 16)
            sp.dma_start(bos[:, :], bo.broadcast_to([P, D])).then_inc(s_w, 16)
            sp.dma_start(xall[:, QT:NT, :], x[SEQ:T, :].rearrange("(t p) d -> p t d", p=P)).then_inc(s_xrest, 16)
            sp.wait_ge(s_padrow, 1)
            with sp.Fori(0, NE) as e:
                sp.dma_start(routed[bass.ds(e * REG, CAP), :].rearrange("(t p) d -> p t d", p=P),
                             pad_rows[:, :, :]).then_inc(prefill_done, 16)
            for t in range(T // CAP + 1):
                n = min(CAP, T - t * CAP) // P
                sp.dma_start(acc[1][t * CAP:t * CAP + n * P, :].rearrange("(t p) d -> p t d", p=P),
                             pad_rows[:, 0:n, 0:D]).then_inc(acc_init, 16)
            for a in acc:
                sp.dma_start(a[T:T + DUMMY, :].rearrange("(t p) d -> p t d", p=P),
                             pad_rows[:, :, 0:D]).then_inc(acc_init, 16)
            for e in range(4):
                sp.dma_start(wexp[e][:, :], experts[e]).then_inc(w_in[e], 16)
            with sp.Fori(0, NB) as b:
                at = sp.snap(b * SEQ)
                tile = sp.snap(b * QT)
                sp.wait_ge(x2_ready, b + 1)
                sp.dma_start(acc[0][bass.ds(at, SEQ), :].rearrange("(t p) d -> p t d", p=P),
                             xb[:, bass.ds(tile, QT), :]).then_inc(acc_init, 16)
            sp.wait_ge(ov_ready, 1)
            sp.dma_start(over_table, ovi[:, :]).then_inc(ov_stored, 16)
            for e in range(4):
                sp.wait_ge(scattered[TOPK - 1 - e], 16 * NT)
                sp.dma_start(xt[e][:, :, :], routed[e * REG:e * REG + CAP, :].rearrange("(t p) d -> p t d", p=P))\
                    .then_inc(xt_in[e], 16)

            for k in range(TOPK - 4):
                sp.wait_ge(scattered[k], 16 * NT)
            with sp.Fori(1, NE // 4) as q:
                for k in range(4):
                    row, wrow = sp.snap((q * 4 + k) * REG), sp.snap((q * 4 + k) * P)
                    used = sp.snap(q * 4 + (k - 3))
                    sp.wait_ge(tw_ready, used)
                    sp.dma_start(xt[k][:, :, :], routed[bass.ds(row, CAP), :].rearrange("(t p) d -> p t d", p=P))\
                        .then_inc(xt_in[k], 16)
                    sp.wait_ge(ob_ps, used)
                    sp.dma_start(wexp[k][:, :], experts.rearrange("e p w -> (e p) w")[bass.ds(wrow, P), :])\
                        .then_inc(w_in[k], 16)
            sp.wait_ge(ov_stored, 16)
            total = sp.value_load(over_table[0:1, 3:4], min_val=0, max_val=MAX_OVER)
            sp.wait_ge(tw_ready, NE - 3)
            sp.wait_ge(ob_ps, NE - 3)
            with sp.If(total > 0):
                with sp.Fori(0, total) as t:
                    row = sp.value_load(over_table[bass.ds(t, 1), 0:1], min_val=0, max_val=NE * REG - P)
                    e = sp.value_load(over_table[bass.ds(t, 1), 1:2], min_val=0, max_val=NE - 1)
                    pad = sp.value_load(over_table[bass.ds(t, 1), 2:3], min_val=0, max_val=NE * REG - P)
                    sp.dma_start(routed[bass.ds(pad, P), :], pad_rows[:, 0, :]).then_inc(v_pad, 16)
                    sp.dma_start(wexp[0][:, :], experts[bass.ds(e, 1)].rearrange("e p w -> (e p) w")).then_inc(v_ld, 16)
                    src, padded = routed[bass.ds(row, P), :], sp.snap(t * 16 + 16)
                    sp.wait_ge(v_pad, padded)
                    sp.dma_start(xt[0][:, 0, :], src).then_inc(v_ld, 16)
                    sp.wait_ge(v_add, t * 16 + 16)
                    carry_wait(sp)
            sp.wait_ge(added[0], 16 * CAPT * NE // 2)
            n, r = NT // 4, T // 4
            for a in range(2):
                if a == 1:
                    sp.wait_ge(added[1], 16 * CAPT * NE // 2)
                for c in range(4):
                    sp.dma_start((xb, rows)[a][:, n * c:n * c + n, 0:D],
                                 acc[a][r * c:r * c + r, :].rearrange("(t p) d -> p t d", p=P)).then_inc(f_in[c], 16)
            for c in range(4):
                sp.wait_ge(f_sum, c + 1)
                sp.dma_start(y[r * c:r * c + r, :].rearrange("(t p) d -> p t d", p=P),
                             xb[:, n * c:n * c + n, :]).then_inc(f_out, 16)
            sp.wait_ge(f_out, 64)
            sp.wait_ge(acc_init, 16 * (T // CAP + 1 + 2 + NB))

        @block.gpsimd
        def _(pool):
            pool.wait_ge(bias_ready, 1)
            pool.wait_ge(s_x0, 16)
            pool.wait_ge(s_xrest, 16)
            for b in range(NB):
                pool.tensor_tensor(xb[:, b * QT:b * QT + QT, :], xall[:, b * QT:b * QT + QT, :],
                                   bos[:, :].unsqueeze(1).broadcast_to([P, QT, D]), ALU.add).then_inc(xb_ready, 1)
            pool.wait_ge(prefill_done, 16 * NE)
            for b in range(NB):
                pool.wait_ge(rowx_ready, b + 1)
                pool.wait_ge(probs_ready, b + 1)
                pool.wait_ge(slots_ready, b + 1)
                for k in reversed(range(TOPK)):
                    for t in range(b * QT, (b + 1) * QT):
                        pool.indirect_dma_start(
                            out=routed, out_offset=bass.IndirectOffsetOnAxis(ap=slots[:, t, k:k + 1], axis=0),
                            in_=rows[:, t, :], in_offset=None).then_inc(scattered[k], 16)
            pool.wait_ge(acc_init, 16 * (T // CAP + 1 + 2 + NB))

            with pool.Fori(0, NE // 4) as q:
                for k in range(4):
                    pool.wait_ge(oa_out, q * 4 + k + 1)
                    pool.wait_ge(ob_out, q * 4 + k + 1)
                    carry_wait(pool)
                    for j in range(CAPT):
                        pool.indirect_dma_start(
                            out=acc[k % 2], out_offset=bass.IndirectOffsetOnAxis(
                                ap=tok[k][:, j:j + 1], axis=0),
                            in_=osb[k % 2][:, j, :], in_offset=None, compute_op=ALU.add).then_inc(added[k % 2], 16)
            pool.wait_ge(ov_stored, 16)
            total = pool.value_load(over_table[0:1, 3:4], min_val=0, max_val=MAX_OVER)
            pool.wait_ge(added[1], 16 * CAPT * NE // 2)
            with pool.If(total > 0):
                with pool.Fori(0, total) as t:
                    pool.wait_ge(v_osb, t + 1)
                    carry_wait(pool)
                    pool.indirect_dma_start(
                        out=acc[1], out_offset=bass.IndirectOffsetOnAxis(
                            ap=xt[0][:, 0, IDC:IDC + 1].bitcast(i32), axis=0),
                        in_=osb[0][:, 0, :], in_offset=None, compute_op=ALU.add).then_inc(v_add, 16)

        @block.tensor
        def _(pe):
            pe.wait_ge(s_prep, 1)
            pe.wait_ge(s_w, 16 * 8)

            def transposes(dst, src, n_tok):
                for c in range(DC):
                    for t in range(n_tok):
                        last = pe.transpose(dst[:, (c * n_tok + t) * P:(c * n_tok + t + 1) * P],
                                            src[:, t, c * P:(c + 1) * P], ident)
                return last

            def xn_transposes(b):
                wait(pe, xn_ready, b + 1)
                transposes(ps_x0, xn, QT).then_inc(xnT_ps, 1)

            def project(dst, w, done):
                for m in range(DC):
                    for c in range(DC):
                        last = pe.matmul(dst[:, m * SEQ:(m + 1) * SEQ], w[:, c, m * P:(m + 1) * P], xnT[:, c, :],
                                         start=(c == 0), stop=(c == DC - 1))
                last.then_inc(done, 1)

            def token_major(dst, src, w, done):
                n = w.shape[2]
                for t in range(QT):
                    for c in range(DC):
                        last = pe.matmul(dst[:, t * n:(t + 1) * n], src[:, c, t * P:(t + 1) * P], w[:, c, :],
                                         start=(c == 0), stop=(c == DC - 1))
                last.then_inc(done, 1)

            def scores(b, par, s, u):
                m, r = s // 4, 32 * (s % 4)
                q, k = qT[par][r:r + 32, m, :], kT[par][r:r + 32, m, :, :]
                if s == 0:
                    wait(pe, q_ready, b + 1)
                    wait(pe, k_ready, b + 1)
                if isinstance(b, int) and u == 0:
                    pe.wait_ge(bias_ready, 1)
                wait(pe, p1_ready, u)
                pe.matmul(ps_s1[:, :], q[:, P:SEQ], k, start=True, stop=False)
                pe.matmul(ps_s1[:, :].rearrange("p (h k) -> p h k", h=2)[:, :, P:SEQ], ident_b[:, :],
                          causal_b[:, :].unsqueeze(1).broadcast_to([P, 2, P]), start=False, stop=True).then_inc(s1_done, 1)
                wait(pe, p0_ready, u)
                pe.matmul(ps_s0[:, 0:2 * P], q[:, 0:P], k[:, :, 0:P], start=True, stop=False)
                pe.matmul(ps_s0[:, 0:2 * P].rearrange("p (h k) -> p h k", h=2), ident_b[:, :],
                          causal_b[:, :].unsqueeze(1).broadcast_to([P, 2, P]), start=False, stop=True).then_inc(s0_done, 1)

            def prob_transposes(s, u):
                wait(pe, p1_ready, u + 1)
                wait(pe, pt1_ready, u)
                for i, (h, kt) in enumerate(((0, 0), (0, 1), (1, 0))):
                    last = pe.transpose(ps_t1[:, i * P:(i + 1) * P], pr1[s % 2][:, h, kt * P:(kt + 1) * P], ident)
                last.then_inc(t1_done, 1)
                wait(pe, p0_ready, u + 1)
                wait(pe, pt0_ready, u)
                pe.transpose(ps_t0[:, 0:P], pr1[s % 2][:, 1, P:2 * P], ident)
                for h in range(2):
                    last = pe.transpose(ps_t0[:, (1 + h) * P:(2 + h) * P], pr0[s % 2][:, h, :], ident)
                last.then_inc(t0_done, 1)

            def values(b, par, s, u):
                if s == 0:
                    wait(pe, attn_ready, b)
                    wait(pe, v_ready, b + 1)
                wait(pe, pt1_ready, u + 1)
                wait(pe, pt0_ready, u + 1)
                for h in range(2):
                    head = 2 * s + h
                    col = slice(head * VW, (head + 1) * VW)
                    pe.matmul(ps_o0[:, col], pt0[s % 2][:, 1 + h, :], vt[par][:, 0, head, :], start=True, stop=True)
                    for kt in range(QT):
                        block = h * QT + kt
                        p_t = pt1[s % 2][:, block, :] if block < 3 else pt0[s % 2][:, 0, :]
                        last = pe.matmul(ps_o1[:, col], p_t, vt[par][:, kt, head, :],
                                         start=(kt == 0), stop=(kt == QT - 1))
                last.then_inc(av_done, 1)

            pe.wait_ge(bvw_ready, 1)
            for c in range(DC):
                last = pe.matmul(ps_s1[:, 0:D], bvw[:, c, :], wos[:, c, :], start=(c == 0), stop=(c == DC - 1))
            last.then_inc(bias_ps, 1)
            xn_transposes(0)
            wait(pe, xnT_ready, 1)
            project(ps_x0, wqs, q_ps)
            token_major(ps_x1, xnT, wvs, v_ps)
            wait(pe, q_ready, 1)
            project(ps_x0, wks, k_ps)
            wait(pe, k_ready, 1)

            def step(b, par, n):
                now, pre, post, old = n < NB, n < NB - 1, 1 <= n <= NB, n >= 2
                for s in range(PAIRS):
                    u = unit(b, s)
                    if now:
                        scores(b, par, s, u)
                    if (now and (n, s) != (0, 0)) or (n == NB and s == 0):
                        prob_transposes(s - 1, u - 1)
                    if s >= 2 and now:
                        values(b, par, s - 2, u - 2)
                    elif s < 2 and post:
                        values(b - 1, 1 - par, s + PAIRS - 2, u - 2)
                    if s == 1 and pre:
                        wait(pe, x2_ready, b - 1)
                        xn_transposes(b + 1)
                    if s == 1 and old:
                        wait(pe, xn2_ready, b - 1)
                        wait(pe, v_ready, min(n, NB - 1) + 1 if isinstance(b, int) else b + 1)
                        transposes(ps_x1, xn2, QT).then_inc(x2T_ps, 1)
                    if s == 2 and pre:
                        wait(pe, xnT_ready, b + 2)
                        project(ps_x0, wqs, q_ps)
                    if s == 2 and old:
                        wait(pe, x2T_ready, b - 1)
                        token_major(ps_x1, x2T, gates, lg_ps)
                    if s == 3 and pre:
                        wait(pe, q_ready, b + 2)
                        project(ps_x0, wks, k_ps)
                    if s == 4 and post:
                        wait(pe, attn_ready, b)
                        if old:
                            wait(pe, lg_read, b - 1)
                        else:
                            wait(pe, v_ready, b + 1)
                        transposes(ps_x1, attn, QT).then_inc(aT_ps, 1)
                    if s == 4 and old:
                        wait(pe, mask_ready, b - 1)
                        if pre:
                            wait(pe, k_ready, b + 2)
                        elif post:
                            wait(pe, x2_ready, b - 1)
                        for t in range(QT):
                            dst = ps_x0[:, t * NE:(t + 1) * NE]
                            pe.matmul(dst, before_b[:, :], chosen[:, t, :], start=True, stop=False)
                            for j in range(t):
                                pe.matmul(dst, ones_b[:, :], chosen[:, j, :], start=False, stop=False)
                            last = pe.matmul(dst, ones_b[:, :], seen[:, :], start=False, stop=True)
                        last.then_inc(rank_ps, 1)
                    if s == 5 and post:
                        wait(pe, aT_ready, b)
                        if old:
                            wait(pe, rank_read, b - 1)
                        elif pre:
                            wait(pe, k_ready, b + 2)
                        token_major(ps_x0, aT, wos, wo_ps)
                    if s == 6 and pre:
                        if post:
                            wait(pe, aT_ready, b)
                        else:
                            wait(pe, v_ready, b + 1)
                        token_major(ps_x1, xnT, wvs, v_ps)

            batches(pe, step)
            pe.wait_ge(slots_ready, NB)
            pe.matmul(ps_x0[:, 0:NE], ones_b[:, :], seen[:, :], start=True, stop=True).then_inc(cnt_ps, 1)

            def x_transposes(src, tiles, done):
                for c in range(DC):
                    for j in range(tiles):
                        last = pe.transpose(ps_tx[c][:, j * P:(j + 1) * P], src[:, j, c * P:(c + 1) * P], ident)
                    last.then_inc(done[c], 1)

            def gate_up(w, src, n, g_done, u_done, u_free):
                for i, (dst, done) in enumerate(((ps_g, g_done), (ps_u, u_done))):
                    if i == 1:
                        u_free()
                    for c in range(DC):
                        at = c * 2 * INTER + i * INTER
                        last = pe.matmul(dst[:, 0:n], w[:, at:at + INTER], src[:, c, 0:n],
                                         start=(c == 0), stop=(c == DC - 1))
                    if done is not None:
                        last.then_inc(done, 1)

            def down(w, h, k, j):
                dst = ps_oa[k][:, j * D:(j + 1) * D] if j < 2 else ps_ob[k][:, 0:D]
                return pe.matmul(dst, h[:, j * P:(j + 1) * P], w[:, DC * 2 * INTER:WW], start=True, stop=True)

            def turn(q, k):
                pe.wait_ge(xt_in[k], (q + 1) * 16)
                for c in range(DC):
                    wait(pe, xT_ready[c], q * 4 + k)
                x_transposes(xt[k], CAPT, tx_ps)

            pe.wait_ge(ov_ready, 1)
            turn(0, 0)

            def expert(q, k, n):
                e = q * 4 + k
                if n < NE - 1:
                    turn(*after(q, k))
                if n < NE:
                    pe.wait_ge(w_in[k], (q + 1) * 16)
                    for c in range(DC):
                        pe.wait_ge(xT_ready[c], e + 1)
                    wait(pe, sg_ready, e)
                    gate_up(wexp[k], xT[k % 2], CAP, g_ps, u_ps, lambda: wait(pe, h_ready, e))
                if n > 0:
                    wait(pe, h_ready, e)
                    wait(pe, oa_out, e - 2)
                    wait(pe, ob_out, e - 2)
                    kk = (k - 1) % 4
                    for j in range(CAPT):
                        o = down(wexp[kk], hT[kk % 2], kk % 2, j)
                        if j == 1:
                            o.then_inc(oa_ps, 1)
                    o.then_inc(ob_ps, 1)

            expert_loop(pe, expert)
            pe.wait_ge(ov_stored, 16)
            total = pe.value_load(over_table[0:1, 3:4], min_val=0, max_val=MAX_OVER)
            with pe.If(total > 0):
                with pe.Fori(0, total) as t:
                    pe.wait_ge(v_ld, t * 32 + 32)
                    for c in range(DC):
                        pe.wait_ge(xT_ready[c], NE)
                    pe.wait_ge(oa_out, NE - 1)
                    for c in range(DC):
                        o = pe.transpose(ps_tx[c][:, 0:P], xt[0][:, 0, c * P:(c + 1) * P], ident)
                    o.then_inc(v_tx, 1)
                    pe.wait_ge(v_xT, t + 1)
                    gate_up(wexp[0], xT[0], P, None, v_gu, lambda: None)
                    pe.wait_ge(v_h, t + 1)
                    down(wexp[0], hT[0], 0, 0).then_inc(v_o, 1)

        @block.scalar
        def _(act):
            act.wait_ge(s_w, 16 * 8)
            act.wait_ge(s_cst, 32)
            for h, mask in enumerate((C_EVEN, C_ODD)):
                act.activation(bkm[:, h, :], bqks[:, DC:2 * DC], ACT.Copy, scale=cst[:, mask:mask + 1])
            act.mul(bqs[:, :], bqks[:, 0:DC], SCALE).then_inc(s_bkm, 1)
            act.wait_ge(s_bkm, 1)

            def copy(dst, src, ready, done, value):
                wait(act, ready, value)
                act.copy(dst, src).then_inc(done, 1)

            def flat(a):
                return a[:, :, :].rearrange("p a b -> p (a b)")

            def q_out(b, par):
                wait(act, q_ps, b + 1)
                for m in range(DC):
                    last = act.activation(qT[par][:, m, :], ps_x0[:, m * SEQ:(m + 1) * SEQ], ACT.Identity,
                                          bias=bqs[:, m:m + 1], scale=SCALE)
                last.then_inc(q_ready, 1)

            def v_out(b, par):
                wait(act, v_ps, b + 1)
                act.copy(vt[par][:, :, :, 0:HD], ps_x1[:, :].rearrange("p (t h d) -> p t h d", t=QT, d=HD))\
                    .then_inc(v_ready, 1)

            def k_out(b, par):
                wait(act, k_ps, b + 1)
                for m in range(DC):
                    for h, mask in enumerate((C_EVEN, C_ODD)):
                        last = act.activation(kT[par][:, m, h, :], ps_x0[:, m * SEQ:(m + 1) * SEQ], ACT.Identity,
                                              bias=bkm[:, h, m:m + 1], scale=cst[:, mask:mask + 1])
                last.then_inc(k_ready, 1)

            copy(flat(xnT), ps_x0[:, :], xnT_ps, xnT_ready, 1)
            q_out(0, 0)
            v_out(0, 0)
            k_out(0, 0)

            def step(b, par, n):
                now, pre, post, old = n < NB, n < NB - 1, 1 <= n <= NB, n >= 2
                for s in range(PAIRS):
                    u = unit(b, s)
                    if now:
                        wait(act, nm1_ready, u + 1)
                        wait(act, t0_done, u - 1)
                        for h in range(2):
                            last = act.activation(pr1[s % 2][:, h, :], ps_s1[:, h * SEQ:(h + 1) * SEQ], ACT.Exp,
                                                  bias=nm[:, s % 2, h:h + 1], scale=1.0)
                        last.then_inc(p1_ready, 1)
                        wait(act, nm0_ready, u + 1)
                        for h in range(2):
                            last = act.activation(pr0[s % 2][:, h, :], ps_s0[:, h * P:(h + 1) * P], ACT.Exp,
                                                  bias=nm[:, s % 2, 2 + h:3 + h], scale=1.0)
                        last.then_inc(p0_ready, 1)
                    if (now and (n, s) != (0, 0)) or (n == NB and s == 0):
                        wait(act, t0_done, u)
                        wait(act, av_done, u - 2)
                        act.copy(flat(pt0[(s - 1) % 2]), ps_t0[:, 0:3 * P]).then_inc(pt0_ready, 1)
                    if s == 1 and old:
                        wait(act, xn2_ready, b - 1)
                        act.copy(rows[:, bass.ds((b - 2) * QT, QT), 0:D], xn2[:, :, :]).then_inc(rowx_ready, 1)
                    if s == 1 and pre:
                        copy(flat(xnT), ps_x0[:, :], xnT_ps, xnT_ready, b + 2)
                    if s == 1 and old:
                        copy(flat(x2T), ps_x1[:, :], x2T_ps, x2T_ready, b - 1)
                    if s == 2 and pre:
                        q_out(b + 1, 1 - par)
                    if s == 3 and pre:
                        k_out(b + 1, 1 - par)
                    if s == 4 and old:
                        wait(act, mask_ready, b - 1)
                        for t in range(QT):
                            last = act.activation(elg[:, t, :], lg[:, t, :], ACT.Exp, bias=nmx[:, t:t + 1], scale=1.0,
                                                  accum_out=esum[:, t:t + 1])
                        last.then_inc(e_ready, 1)
                    if s == 4 and post:
                        copy(flat(aT), ps_x1[:, :], aT_ps, aT_ready, b)
                    if s == 6 and pre:
                        v_out(b + 1, 1 - par)

            batches(act, step)

            def x_out(q, k):
                act.wait_ge(tx_ps[0], q * 4 + k + 1)
                act.copy(xT[k % 2][:, 0, :], ps_tx[0][:, 0:CAP]).then_inc(xT_ready[0], 1)

            x_out(0, 0)

            def expert(q, k, n):
                e = q * 4 + k
                if n < NE - 1:
                    x_out(*after(q, k))
                if n < NE:
                    act.wait_ge(g_ps, e + 1)
                    act.activation(sg[k % 2][:, :], ps_g[:, 0:CAP], ACT.Silu).then_inc(sg_ready, 1)
                if n > 0:
                    kk = (k - 1) % 4
                    act.wait_ge(oa_ps, e)
                    act.wait_ge(tw_ready, e)
                    wait(act, added[kk % 2], earlier_adds(*before(q, k)))
                    for j in range(2):
                        last = act.activation(osb[kk % 2][:, j, :], ps_oa[kk % 2][:, j * D:(j + 1) * D], ACT.Copy,
                                              scale=wgt[kk][:, j:j + 1])
                    last.then_inc(oa_out, 1)

            expert_loop(act, expert)
            act.wait_ge(ov_stored, 16)
            total = act.value_load(over_table[0:1, 3:4], min_val=0, max_val=MAX_OVER)
            with act.If(total > 0):
                with act.Fori(0, total) as t:
                    act.wait_ge(v_gu, t + 1)
                    act.activation(sg[0][:, 0:P], ps_g[:, 0:P], ACT.Silu).then_inc(v_sg, 1)

        @block.vector
        def _(dve):
            dve.wait_ge(s_cst, 32)
            for dst, at in ((ident_b, C_ID), (before_b, C_LT), (causal_b, C_CAUSAL)):
                dve.tensor_copy(dst[:, :], cst[:, at:at + P])
            dve.memset(pad_rows[:, :, :].rearrange("p a b -> p (a b)"), 0.0).then_inc(pad_link, 1)
            for t in vt:
                dve.memset(t[:, :, :, :].rearrange("p a b c -> p (a b c)"), 1.0)
            dve.memset(ones_b[:, :], 1.0)
            dve.memset(onese[:, :], 1.0)
            dve.memset(seen[:, :], 0.0).then_inc(s_prep, 1)
            dve.tensor_copy(rows[:, :, IDC].bitcast(i32), idt[:, CAPT:CAPT + NT])
            dve.wait_ge(pad_link, 1)
            dve.tensor_copy(pad_rows[:, :, IDC].bitcast(i32), idt[:, 0:CAPT]).then_inc(s_padrow, 1)
            dve.wait_ge(s_w, 16 * 8)
            dve.tensor_copy(bvw[:, :, :], bvs[:, :].unsqueeze(2).broadcast_to([P, DC, P])).then_inc(bvw_ready, 1)

            def stats(half, src):
                carry_wait(dve)
                for t in range(QT):
                    last = dve.bn_stats(st6[:, half * QT + t, :], src(t))
                last.then_inc(st_done[half], 1)

            def chain(n, halves, part):
                at = [n * LN_LINKS + (0, LN_CUT, LN_CUT + 3)[part]]
                lo, hi = QT * halves[0], QT * (halves[-1] + 1)
                cols = slice(lo, hi)

                def linked(ins):
                    ins.then_inc(ln_link, 1)
                    at[0] = at[0] + 1
                    dve.wait_ge(ln_link, at[0])

                def newton():
                    linked(dve.tensor_tensor(tn[:, cols], rs[:, cols], rs[:, cols], ALU.mult))
                    linked(dve.tensor_tensor(tn[:, cols], tn[:, cols], hv[:, cols], ALU.mult))
                    linked(dve.scalar_tensor_tensor(rs[:, cols], tn[:, cols], 1.5, rs[:, cols], ALU.add, ALU.mult))

                if part == 0:
                    carry_wait(dve)
                    for c in range(lo, hi):
                        last = dve.bn_aggr(mv[:, c, :], st6[:, c, :])
                    linked(last)
                    dve.tensor_scalar(hv[:, cols], mv[:, cols, 1], EPS, -0.5, ALU.add, ALU.mult)
                    linked(dve.tensor_scalar(ve[:, cols], mv[:, cols, 1], EPS, None, ALU.add))
                    linked(dve.tensor_scalar(rs[:, cols].bitcast(i32), ve[:, cols].bitcast(i32), -0.5,
                                             float(RSQRT_MAGIC), ALU.mult, ALU.add))
                newton()

            def apply(half, src, dst, done):
                for t in range(QT):
                    c = half * QT + t
                    last = dve.tensor_scalar(dst[:, t, :], src(t), mv[:, c, 0:1], rs[:, c:c + 1],
                                             ALU.subtract, ALU.mult)
                last.then_inc(done, 1)

            def rows_of(x, b):
                return lambda t: x[:, b * QT + t, :]

            def norm1(b):
                stats(0, rows_of(xall, b))
                wait(dve, st_done[0], b + 1)
                chain(b, [0], 0)
                chain(b, [0], 1)
                chain(b, [0], 2)
                apply(0, rows_of(xall, b), xn, xn_ready)

            dve.wait_ge(s_x0, 16)
            norm1(0)
            dve.wait_ge(xnT_ps, 1)
            dve.wait_ge(s_xrest, 16)
            norm1(1)
            dve.wait_ge(bias_ps, 1)
            dve.tensor_tensor(bos[:, :], ps_s1[:, 0:D], bos[:, :], ALU.add).then_inc(bias_ready, 1)

            def step(b, par, n):
                now, pre, post, old = n < NB, n < NB - 1, 1 <= n <= NB, n >= 2
                next_ = n < NB - 2
                halves = [0] * next_ + [1] * post
                was = [0] * (pre and n >= 1) + [1] * old
                for s in range(PAIRS):
                    u, sp_ = unit(b, s), s % 2
                    if now:
                        wait(dve, s1_done, u + 1)
                        dve.reduce_max(nm[:, sp_, 0:2], ps_s1[:, :].rearrange("p (h k) -> p h k", h=2),
                                       axis=AX.X, negate=True).then_inc(nm1_ready, 1)
                        wait(dve, s0_done, u + 1)
                        dve.reduce_max(nm[:, sp_, 2:4], ps_s0[:, 0:2 * P].rearrange("p (h k) -> p h k", h=2),
                                       axis=AX.X, negate=True).then_inc(nm0_ready, 1)
                    if (now and (n, s) != (0, 0)) or (n == NB and s == 0):
                        wait(dve, t1_done, u)
                        wait(dve, av_done, u - 2)
                        dve.tensor_copy(pt1[(s - 1) % 2][:, :, :].rearrange("p a b -> p (a b)"), ps_t1[:, 0:3 * P])\
                            .then_inc(pt1_ready, 1)
                    if s == 3 and old:
                        wait(dve, lg_ps, b - 1)
                        dve.tensor_copy(lg[:, :, :].rearrange("p a b -> p (a b)"), ps_x1[:, 0:QT * NE]).then_inc(lg_read, 1)
                        wait(dve, lg_read, b - 1)
                        carry_wait(dve)
                        for t in range(QT):
                            last = dve.max(top[:, t, :], lg[:, t, :])
                        last.then_inc(top_link, 1)
                        wait(dve, top_link, b * 2 - 3)
                        dve.tensor_scalar(nmx[:, :], top[:, :, 0], -1.0, None, ALU.mult)
                        for t in range(QT):
                            last = dve.match_replace(rest[:, t, :], top[:, t, :], lg[:, t, :], -3e38)
                        last.then_inc(top_link, 1)
                        wait(dve, top_link, b * 2 - 2)
                        dve.tensor_tensor(chosen[:, :, :], rest[:, :, :], lg[:, :, :], ALU.is_lt).then_inc(mask_ready, 1)
                    if s == 1 and post:
                        wait(dve, av_done, b * PAIRS)
                        for t, o in enumerate((ps_o0, ps_o1)):
                            last = dve.reciprocal(rden[:, t, :], o[:, 0:NH * VW].rearrange("p (h v) -> p h v", v=VW)[:, :, HD])
                        last.then_inc(norm_link, 1)
                        wait(dve, norm_link, b)
                        for t, o in enumerate((ps_o0, ps_o1)):
                            last = dve.tensor_tensor(
                                attn[:, t, :].rearrange("p (h d) -> p h d", d=HD),
                                o[:, 0:NH * VW].rearrange("p (h v) -> p h v", v=VW)[:, :, 0:HD],
                                rden[:, t, :].unsqueeze(2).broadcast_to([P, NH, HD]), ALU.mult)
                        last.then_inc(attn_ready, 1)
                    if s == 5 and old:
                        wait(dve, e_ready, b - 1)
                        dve.reciprocal(erec[:, :], esum[:, :]).then_inc(pr_link, 1)
                        wait(dve, pr_link, b - 1)
                        for t in range(QT):
                            last = dve.tensor_scalar(rows[:, (b - 2) * QT + t, PRC:RW], elg[:, t, :], erec[:, t:t + 1],
                                                     None, ALU.mult)
                        last.then_inc(probs_ready, 1)
                    if s == 5 and post:
                        wait(dve, wo_ps, b)
                        wait(dve, xb_ready, b)
                        mine = xb[:, bass.ds((b - 1) * QT, QT), :]
                        dve.tensor_tensor(mine, ps_x0[:, :].rearrange("p (t d) -> p t d", d=D), mine, ALU.add)\
                            .then_inc(x2_ready, 1)
                        wait(dve, x2_ready, b)
                        stats(1, rows_of(xb, b - 1))
                    if s == 6 and halves:
                        if next_:
                            wait(dve, st_done[0], b + 3)
                        if post:
                            wait(dve, st_done[1], b)
                        chain(b + 2, halves, 0)
                    if s == 7 and halves:
                        chain(b + 2, halves, 1)
                    if s == 0 and was:
                        chain(b + 1, was, 2)
                        if 0 in was:
                            wait(dve, xnT_ps, b + 1)
                            apply(0, rows_of(xall, b + 1), xn, xn_ready)
                        if old:
                            wait(dve, x2T_ps, b - 2)
                            wait(dve, rowx_ready, b - 2)
                            apply(1, rows_of(xb, b - 2), xn2, xn2_ready)
                    if s == 4 and old:
                        wait(dve, rank_ps, b - 1)
                        dve.tensor_tensor(place[:, :, :], ps_x0[:, 0:QT * NE].rearrange("p (t e) -> p t e", e=NE),
                                          cst[:, C_BASE:C_BASE + NE].unsqueeze(1).broadcast_to([P, QT, NE]),
                                          ALU.add).then_inc(rank_read, 1)
                        dve.tensor_tensor(seen[:, :], seen[:, :], chosen[:, 0, :], ALU.add).then_inc(sl_link, 1)
                        wait(dve, rank_read, b - 1)
                        dve.tensor_tensor(place[:, :, :], place[:, :, :], chosen[:, :, :], ALU.mult).then_inc(sl_link, 1)
                        wait(dve, sl_link, b * 3 - 5)
                        dve.tensor_tensor(seen[:, :], seen[:, :], chosen[:, 1, :], ALU.add)
                        wait(dve, sl_link, b * 3 - 4)
                        carry_wait(dve)
                        for t in range(QT):
                            last = dve.max(slotf[:, t, :], place[:, t, :])
                        last.then_inc(sl_link, 1)
                        wait(dve, sl_link, b * 3 - 3)
                        dve.tensor_scalar(slots[:, bass.ds((b - 2) * QT, QT), :], slotf[:, :, :], -1.0, None,
                                          ALU.add).then_inc(slots_ready, 1)
                    if s == 2 and next_:
                        stats(0, rows_of(xall, b + 2))

            batches(dve, step)

            links = [0]

            def linked(ins):
                ins.then_inc(ov_link, 1)
                links[0] += 1
                dve.wait_ge(ov_link, links[0])

            dve.wait_ge(cnt_ps, 1)
            linked(dve.tensor_copy(cnt[:, :], ps_x0[:, 0:NE]))
            linked(dve.tensor_tensor(gt[:, :, :], cnt[:, :].unsqueeze(2).broadcast_to([P, NE, OVT]),
                                     cst[:, C_THR:C_THR + OVT].unsqueeze(1).broadcast_to([P, NE, OVT]), ALU.is_gt))
            linked(dve.reduce_sum(nov[:, :], gt[:, :, :], axis=AX.X))
            linked(dve.tensor_tensor_scan(cum[:, :], onese[:, :], nov[:, :], 0.0, ALU.mult, ALU.add))
            linked(dve.tensor_scalar(ge[:, :], cum[:, :], cst[:, C_IOTA:C_IOTA + 1], None, ALU.is_le))
            dve.reduce_sum(ovv[:, 1:2], ge[:, :], axis=AX.X)
            linked(dve.tensor_tensor(ge[:, :], ge[:, :], nov[:, :], ALU.mult))
            linked(dve.reduce_sum(ovv[:, 4:5], ge[:, :], axis=AX.X))
            linked(dve.tensor_scalar(eq[:, :], cst[:, C_EIDX:C_EIDX + NE], ovv[:, 1:2], None, ALU.is_equal))
            linked(dve.tensor_tensor(eq[:, :], eq[:, :], cnt[:, :], ALU.mult))
            linked(dve.reduce_sum(ovv[:, 5:6], eq[:, :], axis=AX.X))
            linked(dve.tensor_tensor(ovv[:, 6:7], cst[:, C_IOTA:C_IOTA + 1], ovv[:, 4:5], ALU.subtract))
            linked(dve.tensor_scalar(ovv[:, 6:7], ovv[:, 6:7], float(P), float(CAP), ALU.mult, ALU.add))
            linked(dve.scalar_tensor_tensor(ovv[:, 0:1], ovv[:, 1:2], float(REG), ovv[:, 6:7], ALU.mult, ALU.add))
            linked(dve.scalar_tensor_tensor(ovv[:, 2:3], ovv[:, 1:2], float(REG), ovv[:, 5:6], ALU.mult, ALU.add))
            linked(dve.tensor_copy(ovv[:, 3:4], cum[:, NE - 1:NE]))
            dve.tensor_copy(ovi[:, :], ovv[:, 0:4]).then_inc(ov_ready, 1)

            def x_out(q, k):
                dve.wait_ge(tx_ps[1], q * 4 + k + 1)
                dve.tensor_copy(xT[k % 2][:, 1, :], ps_tx[1][:, 0:CAP]).then_inc(xT_ready[1], 1)

            x_out(0, 0)

            def expert(q, k, n):
                e = q * 4 + k
                if n < NE - 1:
                    x_out(*after(q, k))
                if n < NE:
                    dve.wait_ge(sg_ready, e + 1)
                    dve.wait_ge(u_ps, e + 1)
                    dve.tensor_tensor(hT[k % 2][:, :], sg[k % 2][:, :], ps_u[:, 0:CAP], ALU.mult).then_inc(h_ready, 1)
                    if n >= 4:
                        dve.wait_ge(added[k % 2], earlier_adds(q - 1, k) + 16 * CAPT)
                    dve.tensor_copy(tok[k][:, :], xt[k][:, :, IDC].bitcast(i32))
                    dve.tensor_copy(wgt[k][:, :], xt[k][:, :, bass.ds(e + PRC, 1)].rearrange("p j o -> p (j o)"))\
                        .then_inc(tw_ready, 1)
                if n > 0:
                    kk = (k - 1) % 4
                    dve.wait_ge(tw_ready, e)
                    dve.wait_ge(ob_ps, e)
                    wait(dve, added[kk % 2], earlier_adds(*before(q, k)))
                    dve.tensor_scalar(osb[kk % 2][:, 2, :], ps_ob[kk % 2][:, 0:D],
                                      wgt[kk][:, 2:3], None, ALU.mult).then_inc(ob_out, 1)

            expert_loop(dve, expert)

            dve.wait_ge(ov_stored, 16)
            total = dve.value_load(over_table[0:1, 3:4], min_val=0, max_val=MAX_OVER)
            with dve.If(total > 0):
                with dve.Fori(0, total) as t:
                    e = dve.value_load(over_table[bass.ds(t, 1), 1:2], min_val=0, max_val=NE - 1)
                    dve.wait_ge(v_tx, t + 1)
                    for c in range(DC):
                        last = dve.tensor_copy(xT[0][:, c, 0:P], ps_tx[c][:, 0:P])
                    last.then_inc(v_xT, 1)
                    dve.wait_ge(v_sg, t + 1)
                    dve.tensor_tensor(hT[0][:, 0:P], sg[0][:, 0:P], ps_u[:, 0:P], ALU.mult).then_inc(v_h, 1)
                    dve.wait_ge(added[0], 16 * CAPT * NE // 2)
                    dve.wait_ge(v_o, t + 1)
                    dve.tensor_scalar(osb[0][:, 0, :], ps_oa[0][:, 0:D], xt[0][:, 0, bass.ds(e + PRC, 1)], None,
                                      ALU.mult).then_inc(v_osb, 1)

            for c in range(4):
                n = NT // 4
                mine = xb[:, n * c:n * c + n, :]
                dve.wait_ge(f_in[c], 32)
                dve.tensor_tensor(mine, mine, rows[:, n * c:n * c + n, 0:D], ALU.add).then_inc(f_sum, 1)


def kernel(**inputs):
    import concourse.bacc as bacc
    from concourse import mybir as mb
    from concourse.bass_utils import run_bass_kernel_spmd

    a = {k: np.asarray(v) for k, v in inputs.items()}
    w13, w2 = a["L0_ffn_w13"], a["L0_ffn_w2"]
    w13t = np.transpose(w13.reshape(NE, 2 * INTER, DC, P), (0, 3, 2, 1)).reshape(NE, P, DC * 2 * INTER)
    experts = np.concatenate([w13t, np.transpose(w2, (0, 2, 1))], axis=2)
    bq, bk = a["L0_attn_bq"].reshape(DC, P), a["L0_attn_bk"].reshape(DC, P)
    p = np.arange(P)
    consts = np.zeros((P, C_END), np.float32)
    consts[:, C_ID:C_ID + P] = np.eye(P)
    consts[:, C_LT:C_LT + P] = p[:, None] < p[None, :]
    consts[:, C_CAUSAL:C_CAUSAL + P] = np.where(p[None, :] > p[:, None], LOW, 0.0)
    consts[:, C_BASE:C_BASE + NE] = np.arange(NE) * REG + 1
    consts[:, C_EVEN] = p % 32 < HD
    consts[:, C_ODD] = p % 32 >= HD
    consts[:, C_EIDX:C_EIDX + NE] = np.arange(NE)
    consts[:, C_IOTA] = p
    consts[:, C_THR:C_THR + OVT] = CAP + P * np.arange(OVT)
    ids = np.concatenate([T + p[:, None] + P * np.arange(CAPT), p[:, None] + P * np.arange(NT)], axis=1)
    arrays = {
        "x": a["L0_attn_x"].reshape(T, D),
        "wq": a["L0_attn_wq"].T, "wk": a["L0_attn_wk"].T, "wv": a["L0_attn_wv"].T, "wo": a["L0_attn_wo"].T,
        "bqk": np.stack([*bq, *bk], axis=1), "bv": np.stack([*a["L0_attn_bv"].reshape(DC, P)], axis=1), "bo": a["L0_attn_bo"][None, :],
        "gate": a["L0_ffn_gate_w"].T, "experts": experts, "consts": consts, "ids": ids.astype(np.int32),
    }
    arrays = {k: np.ascontiguousarray(v) for k, v in arrays.items()}
    nc = bacc.Bacc("TRN2", target_bir_lowering=False, num_devices=1)
    args = {k: nc.dram_tensor(k + "_dram", v.shape, mb.dt.from_np(v.dtype), kind="ExternalInput").ap()
            for k, v in arrays.items()}
    args["y"] = nc.dram_tensor("y_dram", (T, D), mb.dt.float32, kind="ExternalOutput").ap()
    program(nc, **args)
    r = run_bass_kernel_spmd(nc, [{k + "_dram": v for k, v in arrays.items()}], core_ids=[0])
    return r.results[0]["y_dram"].reshape(NB, SEQ, D)
```

```python
import numpy as np
import concourse.bass as bass
from concourse import mybir
from contextlib import ExitStack

NB, SEQ, D = 8, 256, 256
NH, HD = 16, 16
NE, TOPK, INTER = 64, 8, 128
P = 128
T = NB * SEQ
NT = T // P
QT = SEQ // P
DC = D // P
PAIRS = NH // 2
PW = 2 * HD
CAPT = 3
PT = 108
CAP = CAPT * PT
REG = T + P
IDC, PRC = D, D + 1
RW = D + 1 + NE
DUMMY = CAPT * P
WW = DC * 2 * INTER + D
EPS = 1e-5
SCALE = float(HD) ** -0.5
LOW = -1e30
RSQRT_MAGIC = 0x5F3759DF
LN_CUT = 6
LN_LINKS = LN_CUT + 2 * 3
OVT = -((CAP - T) // P)
MAX_OVER = 115
STACK = 3 * HD
STACK_DMAS = 16 * 6
HALF = NH // 2
FILLS = (6, 14, 6, 14, 6, 12, 6)
EARLY = 6
VALUES_AT = 4
LOOP_B = (2, 6)
C_ID, C_LT, C_CAUSAL, C_BASE, C_EIDX, C_IOTA, C_THR, C_END = (
    np.cumsum([0, P, P, P, NE, NE, 1, OVT]).tolist())


def program(nc, x, wq, wk, wv, wo, bqk, bv, bo, gate, experts, consts, ids, y):
    fp32, bf16, i32 = mybir.dt.float32, mybir.dt.bfloat16, mybir.dt.int32
    fp32r = mybir.dt.float32r
    ALU, ACT, AX = mybir.AluOpType, mybir.ActivationFunctionType, mybir.AxisListType

    routed = nc.dram_tensor("routed", [NE * REG, RW], fp32, kind="Internal").ap()
    acc = [nc.dram_tensor(f"acc{i}", [T + DUMMY, D], fp32, kind="Internal").ap() for i in range(2)]
    parts = nc.dram_tensor("parts", [2, 2, NH, HD, SEQ], fp32, kind="Internal").ap()
    over_table = nc.dram_tensor("over_table", [P, 4], i32, kind="Internal").ap()

    ctx = ExitStack()
    with ctx:
        def sb(name, shape, dt=fp32):
            return ctx.enter_context(nc.sbuf_tensor(name, shape, dt))

        def sem(name):
            return ctx.enter_context(nc.semaphore(name))

        bank = [ctx.enter_context(nc.psum_tensor(f"bank{i}", [P, 512], fp32)) for i in range(8)]
        ps_s1, ps_s0, ps_t, ps_o, ps_x0, ps_x1 = (bank[0], bank[5]), bank[1], bank[2:4], bank[4], bank[6], bank[7]
        ps_tx, ps_g, ps_u, ps_oa, ps_ob = (bank[0], bank[1]), bank[2], bank[3], (bank[4], bank[6]), (bank[5], bank[7])

        cst = sb("cst", [P, C_END])
        idt = sb("idt", [P, CAPT + NT], i32)
        ident = cst[:, C_ID:C_ID + P]
        ident_b = sb("ident_b", [P, P], bf16)
        before_b = sb("before_b", [P, P], bf16)
        causal_b = sb("causal_b", [P, P], bf16)
        ones_b = sb("ones_b", [P, P], bf16)
        gates = sb("gates", [P, DC, NE])
        bqks = sb("bqks", [P, 2 * DC])
        bqs = sb("bqs", [P, DC])
        bvs = sb("bvs", [P, DC])
        bvw = sb("bvw", [P, DC, P])
        bos = sb("bos", [P, D])
        pad_rows = sb("pad_rows", [P, CAPT, RW])
        xall = sb("xall", [P, NT, D])
        xn = sb("xn", [P, QT, D])
        vt = [sb(f"vt{i}", [P, QT, PAIRS, 2 * PW]) for i in range(2)]
        nm = sb("nm", [P, 2, 4])
        den = [sb(f"den{i}", [P, QT, NH]) for i in range(2)]
        rden = sb("rden", [P, QT, NH])
        rdenw = sb("rdenw", [P, QT, D])
        rdenT = sb("rdenT", [P, DC, SEQ])
        xn2 = sb("xn2", [P, QT, D])
        x2T = sb("x2T", [P, DC, SEQ])
        xb = sb("xb", [P, NT, D])
        st6 = sb("st6", [P, 2 * QT, 6])
        mv = sb("mv", [P, 2 * QT, 2])
        ve, hv, rs, tn = (sb(n, [P, 2 * QT]) for n in ("ve", "hv", "rs", "tn"))
        rows = sb("rows", [P, NT, RW])
        lg = sb("lg", [P, QT, NE])
        top = sb("top", [P, QT, TOPK])
        others = sb("others", [P, QT, NE])
        chosen = sb("chosen", [P, QT, NE], bf16)
        seen = sb("seen", [P, NE], bf16)
        nmx = sb("nmx", [P, QT])
        elg = sb("elg", [P, QT, NE])
        esum = sb("esum", [P, QT])
        erec = sb("erec", [P, QT])
        place = sb("place", [P, QT, NE])
        slotf = sb("slotf", [P, QT, TOPK])
        slots = sb("slots", [P, NT, TOPK], i32)
        cnt = sb("cnt", [P, NE])
        gt = sb("gt", [P, NE, OVT])
        nov = sb("nov", [P, NE])
        onese = sb("onese", [P, NE])
        cum = sb("cum", [P, NE])
        ge = sb("ge", [P, NE])
        eq = sb("eq", [P, NE])
        ovv = sb("ovv", [P, 8])
        ovi = sb("ovi", [P, 4], i32)
        xT = sb("xT", [P, DC, P])
        wexp = [sb(f"wexp{i}", [P, WW]) for i in range(4)]
        xt = [sb(f"xt{i}", [P, CAPT, RW]) for i in range(4)]
        tok = [sb(f"tok{i}", [P, CAPT], i32) for i in range(4)]
        wgt = [sb(f"wgt{i}", [P, CAPT]) for i in range(4)]
        with ExitStack() as early:
            def esb(name, shape, dt=fp32):
                return early.enter_context(nc.sbuf_tensor(name, shape, dt))

            qkT = [esb(n, [P, DC * SEQ]) for n in ("qT", "kT")]
            qkp = [esb(n, [P, 2, DC * SEQ], fp32r) for n in ("q_parts", "k_parts")]
            qs, ks = (esb(n, [STACK, NH, SEQ], fp32r) for n in ("q_stack", "k_stack"))
            wqs, wks, wvs, wos = (esb(n, [P, DC, D]) for n in ("wqs", "wks", "wvs", "wos"))
            raw = (wqs, wks, wvs)
            wqp, wkp, wvp = split = [[esb(f"{n}_{v}", [P, DC, D], fp32r) for v in ("hi", "lo")]
                                     for n in ("wq", "wk", "wv")]
            xnT = [esb(f"xnT_{v}", [P, DC, SEQ], fp32r) for v in ("hi", "lo")]
            aT = esb("aT", [P, DC, SEQ])
            pr1 = [esb(f"pr1_{i}", [P, 2, SEQ]) for i in range(2)]
            pr0 = [esb(f"pr0_{i}", [P, 2, P]) for i in range(2)]
            pt = [[esb(f"pt{h}_{i}", [P, 3 * P]) for i in range(2)] for h in range(2)]
        whi, wlo = ([sb(f"w{n}{i}", [P, WW], fp32r) for i in range(4)] for n in ("hi", "lo"))
        xhi, xlo = ([sb(f"x{n}{i}", [P, DC, CAP], fp32r) for i in range(2)] for n in ("hi", "lo"))
        hhi, hlo = ([sb(f"h{n}{i}", [P, CAP], fp32r) for i in range(2)] for n in ("hi", "lo"))
        sg = [sb(f"sg{i}", [P, CAP]) for i in range(2)]
        hT = [sb(f"hT{i}", [P, CAP]) for i in range(2)]
        osb = [sb(f"osb{i}", [P, CAPT, D]) for i in range(4)]

        s_x0, s_xrest, s_w, s_cst = sem("x_first"), sem("x_rest"), sem("weights_in"), sem("consts_in")
        pad_link, s_held = sem("pad_link"), sem("wait_held")
        s_prep, s_padrow, s_bqs = sem("consts_ready"), sem("pad_row_ready"), sem("query_bias_ready")
        xn_ready, xnT_ps, xnT_ready = sem("xn_ready"), sem("xnT_ps"), sem("xnT_ready")
        xnTh_ready, ws_rounded, ws_split = sem("xnT_rounded"), sem("ws_rounded"), sem("ws_split")
        q_ps, k_ps, v_ps = sem("q_ps"), sem("k_ps"), sem("v_ps")
        v_ready = sem("v_ready")
        qk_ready, qkh_ready, qkl_ready, qk_out = ([sem(f"{n}_{w}") for n in "qk"] for w in ("ready", "rounded", "rest", "out"))
        stacks_in = [sem("stacks0_in"), sem("stacks1_in")]
        s1_done, s0_done = sem("s1_done"), sem("s0_done")
        nm1_ready, nm0_ready = sem("nm1_ready"), sem("nm0_ready")
        p1_ready, p0_ready = sem("p1_ready"), sem("p0_ready")
        t_done, pt_ready = ([sem(f"{n}{h}_{w}") for h in range(2)] for n, w in (("t", "done"), ("pt", "ready")))
        av_done, rden_ready, rden_ps, aT_ready = sem("av_done"), sem("rden_ready"), sem("rden_ps"), sem("aT_ready")
        rdenw_ready, rdenT_ready = sem("rdenw_ready"), sem("rdenT_ready")
        wo_ps, x2_ready, xb_ready = sem("wo_ps"), sem("x2_ready"), sem("xb_ready")
        bvw_ready, bias_ps, bias_ready = sem("bvw_ready"), sem("bias_ps"), sem("bias_ready")
        ln_link, st_done = sem("ln_link"), [sem("st1_done"), sem("st2_done")]
        xn2_ready, x2T_ps, x2T_ready = sem("xn2_ready"), sem("x2T_ps"), sem("x2T_ready")
        lg_ps, lg_read, top_link, mask_ready = sem("lg_ps"), sem("lg_read"), sem("top_link"), sem("mask_ready")
        e_ready, pr_link, probs_ready, rowx_ready = sem("e_ready"), sem("pr_link"), sem("probs_ready"), sem("rowx_ready")
        rank_ps, rank_read, sl_link, slots_ready = sem("rank_ps"), sem("rank_read"), sem("sl_link"), sem("slots_ready")
        prefill_done, acc_init = sem("prefill_done"), sem("acc_init")
        scattered = [sem(f"scattered{k}") for k in range(TOPK)]
        cnt_ps, ov_link, ov_ready, ov_stored = sem("cnt_ps"), sem("ov_link"), sem("ov_ready"), sem("ov_stored")
        w_in = [sem(f"w_in{i}") for i in range(4)]
        xt_in = [sem(f"xt_in{i}") for i in range(4)]
        tx_ps = [sem("tx0_ps"), sem("tx1_ps")]
        xh_ready, xl_ready = ([sem(f"x{n}{c}_ready") for c in range(DC)] for n in "hl")
        wh_ready, wl_ready, hh_ready, hl_ready = sem("wh_ready"), sem("wl_ready"), sem("hh_ready"), sem("hl_ready")
        g_ps, u_ps, sg_ready, h_ready = sem("g_ps"), sem("u_ps"), sem("sg_ready"), sem("h_ready")
        oa_ps, ob_ps, oa_out, ob_out = sem("oa_ps"), sem("ob_ps"), sem("oa_out"), sem("ob_out")
        added, tw_ready = [sem("added0"), sem("added1")], sem("tw_ready")
        v_pad, v_ld, v_tx, v_xT, v_gu, v_sg, v_h = (sem("v_" + n) for n in ("pad", "ld", "tx", "xT", "gu", "sg", "h"))
        v_o, v_osb, v_add = sem("v_o"), sem("v_osb"), sem("v_add")
        f_in, f_sum, f_out = [sem(f"f_in{i}") for i in range(4)], sem("f_sum"), sem("f_out")

        block = ctx.enter_context(nc.Block())

        def wait(eng, s, value):
            if not isinstance(value, int) or value > 0:
                eng.wait_ge(s, value)

        def carry_wait(eng):
            eng.sem_inc(s_held, 1)

        def batches(eng, step):
            lo, hi = LOOP_B
            for b in range(lo):
                step(b, b % 2, b)
            with eng.Fori(0, (hi - lo) // 2) as i:
                step(i * 2 + lo, 0, lo)
                step(i * 2 + lo + 1, 1, lo)
            for b in range(hi, NB + 2):
                step(b, b % 2, b)

        def expert_loop(eng, step):
            for k in range(4):
                step(0, k, k)
            with eng.Fori(1, NE // 4 - 1) as q:
                for k in range(4):
                    step(q, k, 4 + k)
            for e in range(NE - 4, NE + 1):
                step(e // 4, e % 4, e)

        def before(q, k):
            return (q, k - 1) if k else (q - 1, 3)

        def after(q, k):
            return (q, k + 1) if k < 3 else (q + 1, 0)

        def earlier_adds(q, k):
            return (q * 2 + k // 2) * (16 * CAPT)

        def unit(b, s):
            return b * PAIRS + s

        @block.sync
        def _(sp):
            sp.dma_start(xall[:, 0:QT, :], x[0:SEQ, :].rearrange("(t p) d -> p t d", p=P)).then_inc(s_x0, 16)
            sp.dma_start(cst[:, :], consts).then_inc(s_cst, 16)
            sp.dma_start(idt[:, :], ids).then_inc(s_cst, 16)
            for dst, src in ((wqs, wq), (wks, wk), (wvs, wv), (wos, wo), (gates, gate)):
                sp.dma_start(dst[:, :, :], src.rearrange("(c p) o -> p c o", p=P)).then_inc(s_w, 16)
            sp.dma_start(bqks[:, :], bqk).then_inc(s_w, 16)
            sp.dma_start(bvs[:, :], bv).then_inc(s_w, 16)
            sp.dma_start(bos[:, :], bo.broadcast_to([P, D])).then_inc(s_w, 16)
            sp.dma_start(xall[:, QT:NT, :], x[SEQ:T, :].rearrange("(t p) d -> p t d", p=P)).then_inc(s_xrest, 16)
            sp.wait_ge(s_padrow, 1)

            def fill(first, n):
                with sp.Fori(first, first + n) as e:
                    sp.dma_start(routed[bass.ds(e * REG, CAP), :].rearrange("(t p) d -> p t d", p=PT),
                                 pad_rows[0:PT, :, :]).then_inc(prefill_done, 16)

            def held(s, value):
                wait(sp, s, value)
                if not isinstance(value, int):
                    carry_wait(sp)

            def parts_out(b):
                held(stacks_in[1], b * STACK_DMAS)
                for i in range(2):
                    held(qkl_ready[i], b + 1)
                    sp.dma_start(parts[i].rearrange("v (c h) d t -> (h d) v c t", c=DC),
                                 qkp[i][:, :, :].bitcast(fp32).rearrange("p v (c t) -> p v c t", c=DC)).then_inc(qk_out[i], 16)

            def stacks(b, half):
                held(s0_done, unit(b - 1, (half + 1) * PAIRS // 2))
                heads = slice(half * HALF, (half + 1) * HALF)
                for i, (dst, vs) in enumerate(((qs, (0, 1, 0)), (ks, (0, 0, 1)))):
                    held(qk_out[i], b * 16 + 16)
                    for g, v in enumerate(vs):
                        sp.dma_start(dst[g * HD:(g + 1) * HD, heads, :].bitcast(fp32),
                                     parts[i, v, heads].rearrange("h d t -> d h t")).then_inc(stacks_in[half], 16)

            def residual(b):
                at, tile = (sp.snap(b * SEQ), sp.snap(b * QT)) if not isinstance(b, int) else (b * SEQ, b * QT)
                held(x2_ready, b + 1)
                sp.dma_start(acc[0][bass.ds(at, SEQ), :].rearrange("(t p) d -> p t d", p=P),
                             xb[:, bass.ds(tile, QT), :]).then_inc(acc_init, 16)

            firsts, peeled = [sum(FILLS[:i]) for i in range(len(FILLS))], len(FILLS) // 2
            fill(0, FILLS[0])
            parts_out(0)
            stacks(0, 0)
            stacks(0, 1)
            for b in range(peeled):
                fill(firsts[2 * b + 1], FILLS[2 * b + 1])
                parts_out(b + 1)
                stacks(b + 1, 0)
                if b >= 1:
                    residual(b - 1)
                fill(firsts[2 * b + 2], FILLS[2 * b + 2])
                stacks(b + 1, 1)
            for t in range(0, NT, 2):
                sp.dma_start(acc[1][t * P:(t + 2) * P, :].rearrange("(t p) d -> p t d", p=P),
                             pad_rows[:, 0:2, 0:D]).then_inc(acc_init, 16)
            for a in acc:
                sp.dma_start(a[T:T + DUMMY, :].rearrange("(t p) d -> p t d", p=P),
                             pad_rows[:, :, 0:D]).then_inc(acc_init, 16)
            with sp.Fori(peeled, NB - 1) as b:
                parts_out(b + 1)
                stacks(b + 1, 0)
                residual(b - 1)
                stacks(b + 1, 1)
            for b in range(NB - 2, NB):
                residual(b)
            for e in range(4):
                sp.dma_start(wexp[e][:, :], experts[e]).then_inc(w_in[e], 16)
            for e in range(4):
                sp.wait_ge(scattered[TOPK - 1 - e], 16 * NT)
                sp.dma_start(xt[e][0:PT, :, :], routed[e * REG:e * REG + CAP, :].rearrange("(t p) d -> p t d", p=PT))\
                    .then_inc(xt_in[e], 16)

            sp.wait_ge(ov_ready, 1)
            sp.dma_start(over_table, ovi[:, :]).then_inc(ov_stored, 16)

            def load(q, k):
                row, wrow = (q * 4 + k) * REG, (q * 4 + k) * P
                used = q * 4 + (k - 3)
                if not isinstance(q, int):
                    row, wrow, used = sp.snap(row), sp.snap(wrow), sp.snap(used)
                sp.wait_ge(wl_ready, used)
                sp.dma_start(wexp[k][:, :], experts.rearrange("e p w -> (e p) w")[bass.ds(wrow, P), :])\
                    .then_inc(w_in[k], 16)
                if isinstance(q, int):
                    sp.wait_ge(scattered[TOPK - 5 - k], 16 * NT)
                sp.wait_ge(tw_ready, used)
                sp.dma_start(xt[k][0:PT, :, :], routed[bass.ds(row, CAP), :].rearrange("(t p) d -> p t d", p=PT))\
                    .then_inc(xt_in[k], 16)

            for k in range(4):
                load(1, k)
            with sp.Fori(2, NE // 4) as q:
                for k in range(4):
                    load(q, k)
            sp.wait_ge(ov_stored, 16)
            total = sp.value_load(over_table[0:1, 3:4], min_val=0, max_val=MAX_OVER)
            sp.wait_ge(tw_ready, NE - 3)
            sp.wait_ge(wl_ready, NE - 3)
            with sp.If(total > 0):
                with sp.Fori(0, total) as t:
                    row = sp.value_load(over_table[bass.ds(t, 1), 0:1], min_val=0, max_val=NE * REG - P)
                    e = sp.value_load(over_table[bass.ds(t, 1), 1:2], min_val=0, max_val=NE - 1)
                    pad = sp.value_load(over_table[bass.ds(t, 1), 2:3], min_val=0, max_val=NE * REG - P)
                    sp.dma_start(routed[bass.ds(pad, P), :], pad_rows[:, 0, :]).then_inc(v_pad, 16)
                    sp.dma_start(wexp[0][:, :], experts[bass.ds(e, 1)].rearrange("e p w -> (e p) w")).then_inc(v_ld, 16)
                    src, padded = routed[bass.ds(row, P), :], sp.snap(t * 16 + 16)
                    sp.wait_ge(v_pad, padded)
                    sp.dma_start(xt[0][:, 0, :], src).then_inc(v_ld, 16)
                    sp.wait_ge(v_add, t * 16 + 16)
                    carry_wait(sp)
            n, r = NT // 4, T // 4
            sp.wait_ge(added[1], 16 * CAPT * NE // 2)
            for c in range(4):
                sp.dma_start(rows[:, n * c:n * c + n, 0:D],
                             acc[1][r * c:r * c + r, :].rearrange("(t p) d -> p t d", p=P)).then_inc(f_in[c], 16)
            for c in range(4):
                sp.wait_ge(f_sum, c + 1)
                sp.dma_start(y[r * c:r * c + r, :].rearrange("(t p) d -> p t d", p=P),
                             xb[:, n * c:n * c + n, :]).then_inc(f_out, 16)
            sp.wait_ge(f_out, 64)
            sp.wait_ge(acc_init, 16 * (NT // 2 + 2 + NB))

        @block.gpsimd
        def _(pool):
            for i, (part, whole) in enumerate(zip(split, raw)):
                pool.wait_ge(ws_rounded, i + 1)
                pool.tensor_tensor(part[1][:, :, :], whole[:, :, :], part[0][:, :, :].bitcast(fp32), ALU.subtract)\
                    .then_inc(ws_split, 1)
            pool.wait_ge(bias_ready, 1)
            pool.wait_ge(s_x0, 16)
            pool.wait_ge(s_xrest, 16)
            for b in range(NB):
                pool.tensor_tensor(xb[:, b * QT:b * QT + QT, :], xall[:, b * QT:b * QT + QT, :],
                                   bos[:, :].unsqueeze(1).broadcast_to([P, QT, D]), ALU.add).then_inc(xb_ready, 1)
            pool.wait_ge(prefill_done, 16 * NE)
            def routable(b):
                pool.wait_ge(rowx_ready, b + 1)
                pool.wait_ge(probs_ready, b + 1)
                pool.wait_ge(slots_ready, b + 1)

            def scatter(b, ks):
                for k in ks:
                    for t in range(b * QT, (b + 1) * QT):
                        pool.indirect_dma_start(
                            out=routed, out_offset=bass.IndirectOffsetOnAxis(ap=slots[:, t, k:k + 1], axis=0),
                            in_=rows[:, t, :], in_offset=None).then_inc(scattered[k], 16)

            def add(q, k):
                pool.wait_ge(oa_out, q * 4 + k + 1)
                pool.wait_ge(ob_out, q * 4 + k + 1)
                wait(pool, added[k % 2], earlier_adds(q, k))
                carry_wait(pool)
                for j in range(CAPT):
                    pool.indirect_dma_start(
                        out=acc[k % 2], out_offset=bass.IndirectOffsetOnAxis(
                            ap=tok[k][0:PT, j:j + 1], axis=0),
                        in_=osb[k][0:PT, j, :], in_offset=None, compute_op=ALU.add).then_inc(added[k % 2], 16)

            order = list(reversed(range(TOPK)))
            for b in range(NB - 2):
                routable(b)
                scatter(b, order)
            routable(NB - 2)
            scatter(NB - 2, order[:EARLY])
            routable(NB - 1)
            scatter(NB - 1, order[:EARLY])
            pool.wait_ge(acc_init, 16 * (NT // 2 + 2 + NB))
            for i, k in enumerate(order[EARLY:]):
                for b in range(NB - 2, NB):
                    scatter(b, [k])
                if i > 0:
                    add(0, i - 1)
            for k in range(TOPK - EARLY - 1, 4):
                add(0, k)
            with pool.Fori(1, NE // 4) as q:
                for k in range(4):
                    add(q, k)
            pool.wait_ge(ov_stored, 16)
            total = pool.value_load(over_table[0:1, 3:4], min_val=0, max_val=MAX_OVER)
            pool.wait_ge(added[1], 16 * CAPT * NE // 2)
            with pool.If(total > 0):
                with pool.Fori(0, total) as t:
                    pool.wait_ge(v_osb, t + 1)
                    carry_wait(pool)
                    pool.indirect_dma_start(
                        out=acc[1], out_offset=bass.IndirectOffsetOnAxis(
                            ap=xt[0][:, 0, IDC:IDC + 1].bitcast(i32), axis=0),
                        in_=osb[0][:, 0, :], in_offset=None, compute_op=ALU.add).then_inc(v_add, 16)

        @block.tensor
        def _(pe):
            pe.wait_ge(s_cst, 32)
            pe.wait_ge(s_w, 16 * 8)

            def transposes(dst, src, n_tok):
                for c in range(DC):
                    for t in range(n_tok):
                        last = pe.transpose(dst[:, (c * n_tok + t) * P:(c * n_tok + t + 1) * P],
                                            src[:, t, c * P:(c + 1) * P], ident)
                return last

            def xn_transposes(b):
                wait(pe, xn_ready, b + 1)
                transposes(ps_x0, xn, QT).then_inc(xnT_ps, 1)

            TERMS = ((0, 0), (0, 1), (1, 0))

            def project(dst, w, done):
                for m in range(DC):
                    for c in range(DC):
                        for i, j in TERMS:
                            last = pe.matmul(dst[:, m * SEQ:(m + 1) * SEQ], w[i][:, c, m * P:(m + 1) * P], xnT[j][:, c, :],
                                             start=(c == i == j == 0), stop=(c == DC - 1 and i == 1))
                last.then_inc(done, 1)

            def token_major(dst, src, w, done):
                for t in range(QT):
                    for c in range(DC):
                        for i, j in TERMS:
                            last = pe.matmul(dst[:, t * D:(t + 1) * D], src[i][:, c, t * P:(t + 1) * P], w[j][:, c, :],
                                             start=(c == i == j == 0), stop=(c == DC - 1 and i == 1))
                last.then_inc(done, 1)

            def plain_token_major(dst, src, w, done):
                n = w.shape[2]
                for t in range(QT):
                    for c in range(DC):
                        last = pe.matmul(dst[:, t * n:(t + 1) * n], src[:, c, t * P:(t + 1) * P], w[:, c, :],
                                         start=(c == 0), stop=(c == DC - 1))
                last.then_inc(done, 1)

            def masked_products(dst, s, queries, n, tail, done):
                for h in range(2):
                    pe.matmul(dst[:, h * n:(h + 1) * n], qs[:, 2 * s + h, queries], ks[:, 2 * s + h, 0:n],
                              start=True, stop=False)
                    last = pe.matmul(dst[:, h * n + tail:(h + 1) * n], ident_b[:, :], causal_b[:, :],
                                     start=False, stop=True)
                last.then_inc(done, 1)

            def scores1(b, s, u):
                if s % (PAIRS // 2) == 0:
                    wait(pe, stacks_in[s // (PAIRS // 2)], (b + 1) * STACK_DMAS)
                if isinstance(b, int) and u == 0:
                    pe.wait_ge(bias_ready, 1)
                wait(pe, p1_ready, u - 1)
                masked_products(ps_s1[s % 2], s, slice(P, SEQ), SEQ, P, s1_done)

            def scores0(s, u):
                wait(pe, p0_ready, u)
                masked_products(ps_s0, s, slice(0, P), P, 0, s0_done)

            def prob_transposes(s, u):
                for h in range(2):
                    wait(pe, p1_ready, u + 1)
                    wait(pe, pt_ready[h], u)
                    for kt in range(QT):
                        pe.transpose(ps_t[h][:, (1 + kt) * P:(2 + kt) * P], pr1[s % 2][:, h, kt * P:(kt + 1) * P], ident)
                    wait(pe, p0_ready, u + 1)
                    pe.transpose(ps_t[h][:, 0:P], pr0[s % 2][:, h, :], ident).then_inc(t_done[h], 1)

            def values(b, par, s, u):
                if s == 0:
                    wait(pe, aT_ready, b)
                    wait(pe, v_ready, b + 1)
                m, r = s // 4, PW * (s % 4)
                for h in range(2):
                    wait(pe, pt_ready[h], u + 1)
                for n, (h, kt, q) in enumerate(((0, 0, 0), (0, 1, P), (1, 1, P), (1, 0, 0))):
                    last = pe.matmul(ps_o[r:r + PW, m * SEQ + q:(m + 1) * SEQ],
                                     vt[par][:, kt, s, h * PW:(h + 1) * PW],
                                     pt[h][s % 2][:, kt * SEQ:kt * SEQ + SEQ - q], start=(n == 0), stop=(n == 3))
                last.then_inc(av_done, 1)

            xn_transposes(0)
            wait(pe, xnT_ready, 1)
            pe.wait_ge(ws_split, 1)
            project(ps_x0, wqp, q_ps)
            wait(pe, qk_ready[0], 1)
            pe.wait_ge(ws_split, 2)
            project(ps_x0, wkp, k_ps)
            pe.wait_ge(ws_split, 3)
            token_major(ps_x1, xnT, wvp, v_ps)
            wait(pe, qk_ready[1], 1)
            pe.wait_ge(bvw_ready, 1)
            for c in range(DC):
                last = pe.matmul(ps_s1[0][:, 0:D], bvw[:, c, :], wos[:, c, :], start=(c == 0), stop=(c == DC - 1))
            last.then_inc(bias_ps, 1)
            pe.wait_ge(s_prep, 1)

            def step(b, par, n):
                now, pre, post, old = n < NB, n < NB - 1, 1 <= n <= NB, n >= 2
                for s in range(PAIRS):
                    u = unit(b, s)
                    if now:
                        scores1(b, s, u)
                        scores0(s, u)
                    if (now and (n, s) != (0, 0)) or (n == NB and s == 0):
                        prob_transposes(s - 1, u - 1)
                    if s >= 2 and now:
                        values(b, par, s - 2, u - 2)
                    elif s < 2 and post:
                        values(b - 1, 1 - par, s + PAIRS - 2, u - 2)
                    if s == 0 and old:
                        wait(pe, x2T_ready, b - 1)
                        if now:
                            wait(pe, v_ready, b + 1)
                        else:
                            wait(pe, rank_read, b - 2)
                        plain_token_major(ps_x1, x2T, gates, lg_ps)
                    if s == 0 and pre:
                        if post:
                            wait(pe, x2T_ready, b - 1)
                        xn_transposes(b + 1)
                    if s == 1 and post:
                        wait(pe, rdenw_ready, b)
                        if old:
                            wait(pe, lg_read, b - 1)
                        else:
                            wait(pe, v_ready, b + 1)
                        transposes(ps_x1, rdenw, QT).then_inc(rden_ps, 1)
                    if s == 1 and pre:
                        wait(pe, xnT_ready, b + 2)
                        project(ps_x0, wqp, q_ps)
                    if s == 2 and pre:
                        wait(pe, qk_ready[0], b + 2)
                        project(ps_x0, wkp, k_ps)
                    if s == 2 and old:
                        wait(pe, mask_ready, b - 1)
                        if post:
                            wait(pe, rdenT_ready, b)
                        else:
                            wait(pe, lg_read, b - 1)
                        for t in range(QT):
                            dst = ps_x1[:, t * NE:(t + 1) * NE]
                            pe.matmul(dst, before_b[:, :], chosen[:, t, :], start=True, stop=False)
                            for j in range(t):
                                pe.matmul(dst, ones_b[:, :], chosen[:, j, :], start=False, stop=False)
                            last = pe.matmul(dst, ones_b[:, :], seen[:, :], start=False, stop=True)
                        last.then_inc(rank_ps, 1)
                    if s == 3 and post:
                        wait(pe, aT_ready, b)
                        if pre:
                            wait(pe, qk_ready[1], b + 2)
                        else:
                            wait(pe, x2T_ready, b - 1)
                        plain_token_major(ps_x0, aT, wos, wo_ps)
                    if s == 7 and post:
                        wait(pe, xn2_ready, b)
                        wait(pe, x2_ready, b)
                        transposes(ps_x0, xn2, QT).then_inc(x2T_ps, 1)
                    if s == VALUES_AT and pre:
                        if old:
                            wait(pe, rank_read, b - 1)
                        elif post:
                            wait(pe, rdenT_ready, b)
                        else:
                            wait(pe, v_ready, b + 1)
                        token_major(ps_x1, xnT, wvp, v_ps)

            batches(pe, step)
            pe.wait_ge(slots_ready, NB)
            pe.matmul(ps_x0[:, 0:NE], ones_b[:, :], seen[:, :], start=True, stop=True).then_inc(cnt_ps, 1)

            def split_product(dst, w_at, x_at, w_parts, x_parts, chunks, swap=False):
                for c in range(chunks):
                    for i, j in TERMS:
                        a, b = w_parts[i][w_at(c)], x_parts[j][x_at(c)]
                        if swap:
                            a, b = b, a
                        last = pe.matmul(dst, a, b, start=(c == i == j == 0), stop=(c == chunks - 1 and i == 1))
                return last

            def turn(q, k):
                pe.wait_ge(xt_in[k], (q + 1) * 16)
                for c in range(DC):
                    wait(pe, xl_ready[c], q * 4 + k)
                for c in range(DC):
                    for j in range(CAPT):
                        last = pe.transpose(ps_tx[c][:, j * PT:(j + 1) * PT], xt[k][0:PT, j, c * P:(c + 1) * P],
                                            ident[0:PT, 0:PT])
                    last.then_inc(tx_ps[c], 1)

            turn(0, 0)

            def expert(q, k, n):
                e = q * 4 + k
                if n < NE - 1:
                    turn(*after(q, k))
                if n < NE:
                    pe.wait_ge(wl_ready, e + 1)
                    for c in range(DC):
                        pe.wait_ge(xl_ready[c], e + 1)
                    wait(pe, sg_ready, e)
                    for i, (dst, done) in enumerate(((ps_g, g_ps), (ps_u, u_ps))):
                        if i == 1:
                            wait(pe, h_ready, e)
                        split_product(dst[:, 0:CAP],
                                      lambda c: (slice(None), slice((2 * c + i) * INTER, (2 * c + i + 1) * INTER)),
                                      lambda c: (slice(None), c, slice(0, CAP)),
                                      (whi[k], wlo[k]), (xhi[k % 2], xlo[k % 2]), DC).then_inc(done, 1)
                if n > 0:
                    wait(pe, hl_ready, e)
                    wait(pe, oa_out, e - 2)
                    wait(pe, ob_out, e - 2)
                    kk = (k - 1) % 4
                    for j in range(CAPT):
                        dst = ps_oa[kk % 2][0:PT, j * D:(j + 1) * D] if j < 2 else ps_ob[kk % 2][0:PT, 0:D]
                        o = split_product(dst, lambda c: (slice(None), slice(DC * 2 * INTER, WW)),
                                          lambda c: (slice(None), slice(j * PT, (j + 1) * PT)),
                                          (whi[kk], wlo[kk]), (hhi[kk % 2], hlo[kk % 2]), 1, swap=True)
                        if j == 1:
                            o.then_inc(oa_ps, 1)
                    o.then_inc(ob_ps, 1)

            expert_loop(pe, expert)
            pe.wait_ge(ov_stored, 16)
            total = pe.value_load(over_table[0:1, 3:4], min_val=0, max_val=MAX_OVER)
            with pe.If(total > 0):
                with pe.Fori(0, total) as t:
                    pe.wait_ge(v_ld, t * 32 + 32)
                    for c in range(DC):
                        pe.wait_ge(xl_ready[c], NE)
                    pe.wait_ge(oa_out, NE - 1)
                    for c in range(DC):
                        o = pe.transpose(ps_tx[c][:, 0:P], xt[0][:, 0, c * P:(c + 1) * P], ident)
                    o.then_inc(v_tx, 1)
                    pe.wait_ge(v_xT, t + 1)
                    for i, dst in enumerate((ps_g, ps_u)):
                        for c in range(DC):
                            at = (2 * c + i) * INTER
                            o = pe.matmul(dst[:, 0:P], wexp[0][:, at:at + INTER], xT[:, c, :],
                                          start=(c == 0), stop=(c == DC - 1))
                    o.then_inc(v_gu, 1)
                    pe.wait_ge(v_h, t + 1)
                    pe.matmul(ps_oa[0][:, 0:D], hT[0][:, 0:P], wexp[0][:, DC * 2 * INTER:WW],
                              start=True, stop=True).then_inc(v_o, 1)

        @block.scalar
        def _(act):
            act.wait_ge(s_w, 16 * 8)
            act.wait_ge(s_cst, 32)
            act.mul(bqs[:, :], bqks[:, 0:DC], SCALE).then_inc(s_bqs, 1)
            act.wait_ge(s_bqs, 1)

            for part, whole in zip(split, raw):
                act.copy(part[0][:, :, :], whole[:, :, :]).then_inc(ws_rounded, 1)

            def copy(dst, src, ready, done, value):
                wait(act, ready, value)
                act.copy(dst, src).then_inc(done, 1)

            def flat(a):
                return a[:, :, :].rearrange("p a b -> p (a b)")

            def qk_out_of_ps(i, b):
                wait(act, (q_ps, k_ps)[i], b + 1)
                wait(act, qkl_ready[i], b)
                for m in range(DC):
                    cols = slice(m * SEQ, (m + 1) * SEQ)
                    bias = bqks[:, DC + m:DC + m + 1] if i else bqs[:, m:m + 1]
                    last = act.activation(qkT[i][:, cols], ps_x0[:, cols], ACT.Identity,
                                          bias=bias, scale=1.0 if i else SCALE)
                last.then_inc(qk_ready[i], 1)
                wait(act, qk_ready[i], b + 1)
                wait(act, qk_out[i], b * 16)
                act.copy(qkp[i][:, 0, :], qkT[i][:, :]).then_inc(qkh_ready[i], 1)

            def v_out(b, par):
                wait(act, v_ps, b + 1)
                act.copy(vt[par][:, :, :, :].rearrange("p t s (a d) -> p (t s) a d", d=HD)[:, :, 0:4:3, :],
                         ps_x1[:, :].rearrange("p (s h d) -> p s h d", h=2, d=HD))\
                    .then_inc(v_ready, 1)

            copy(flat(xnT[0]), ps_x0[:, :], xnT_ps, xnTh_ready, 1)
            qk_out_of_ps(0, 0)
            qk_out_of_ps(1, 0)
            v_out(0, 0)

            def step(b, par, n):
                now, pre, post, old = n < NB, n < NB - 1, 1 <= n <= NB, n >= 2
                for s in range(PAIRS):
                    u = unit(b, s)
                    def exponentials(dst, src, n, maxima, tile, done):
                        for h in range(2):
                            last = act.activation(dst[s % 2][:, h, :], src[:, h * n:(h + 1) * n], ACT.Exp,
                                                  bias=nm[:, s % 2, maxima + h:maxima + h + 1], scale=1.0,
                                                  accum_out=den[par][:, tile, 2 * s + h:2 * s + h + 1])
                        last.then_inc(done, 1)

                    if now:
                        wait(act, nm1_ready, u + 1)
                        wait(act, t_done[1], u - 1)
                        if s == 0:
                            wait(act, rden_ready, b - 1)
                        exponentials(pr1, ps_s1[s % 2], SEQ, 0, 1, p1_ready)
                        wait(act, nm0_ready, u + 1)
                        exponentials(pr0, ps_s0, P, 2, 0, p0_ready)
                    if (now and (n, s) != (0, 0)) or (n == NB and s == 0):
                        wait(act, t_done[1], u)
                        wait(act, av_done, u - 2)
                        act.copy(pt[1][(s - 1) % 2][:, :], ps_t[1][:, 0:3 * P]).then_inc(pt_ready[1], 1)
                    if s == 0 and post:
                        wait(act, rden_ready, b)
                        wait(act, rden_ps, b - 1)
                        act.copy(rdenw[:, :, :].rearrange("p t (h d) -> p (t h) d", d=HD),
                                 rden[:, :, :].rearrange("p t h -> p (t h)").unsqueeze(2)
                                 .broadcast_to([P, QT * NH, HD])).then_inc(rdenw_ready, 1)
                    if s == 0 and pre:
                        copy(flat(xnT[0]), ps_x0[:, :], xnT_ps, xnTh_ready, b + 2)
                    if s == 1 and post:
                        wait(act, aT_ready, b - 1)
                        copy(flat(rdenT), ps_x1[:, :], rden_ps, rdenT_ready, b)
                    if s == 1 and pre:
                        qk_out_of_ps(0, b + 1)
                    if s == 2 and pre:
                        qk_out_of_ps(1, b + 1)
                    if s == 2 and old:
                        wait(act, mask_ready, b - 1)
                        for t in range(QT):
                            last = act.activation(elg[:, t, :], lg[:, t, :], ACT.Exp, bias=nmx[:, t:t + 1], scale=1.0,
                                                  accum_out=esum[:, t:t + 1])
                        last.then_inc(e_ready, 1)
                    if s == 7 and post:
                        wait(act, xn2_ready, b)
                        act.copy(rows[:, bass.ds((b - 1) * QT, QT), 0:D], xn2[:, :, :]).then_inc(rowx_ready, 1)
                    if s == 7 and post:
                        copy(flat(x2T), ps_x0[:, :], x2T_ps, x2T_ready, b)
                    if s == VALUES_AT and pre:
                        v_out(b + 1, 1 - par)

            batches(act, step)

            def x_out(q, k):
                for c in range(DC):
                    act.wait_ge(tx_ps[c], q * 4 + k + 1)
                    wait(act, u_ps, q * 4 + (k - 1))
                    act.copy(xhi[k % 2][:, c, :], ps_tx[c][:, 0:CAP]).then_inc(xh_ready[c], 1)

            def w_out(q, k):
                act.wait_ge(w_in[k], (q + 1) * 16)
                wait(act, ob_ps, q * 4 + (k - 3))
                act.copy(whi[k][:, :], wexp[k][:, :]).then_inc(wh_ready, 1)

            x_out(0, 0)
            w_out(0, 0)
            w_out(0, 1)

            def expert(q, k, n):
                e = q * 4 + k
                if n < NE - 1:
                    x_out(*after(q, k))
                if n < NE:
                    act.wait_ge(g_ps, e + 1)
                    act.activation(sg[k % 2][:, :], ps_g[:, 0:CAP], ACT.Silu).then_inc(sg_ready, 1)
                if n < NE - 2:
                    w_out(*after(*after(q, k)))
                if n < NE:
                    act.wait_ge(h_ready, e + 1)
                    wait(act, ob_ps, e - 1)
                    act.copy(hhi[k % 2][:, :], hT[k % 2][:, :]).then_inc(hh_ready, 1)
                if n > 0:
                    kk = (k - 1) % 4
                    act.wait_ge(oa_ps, e)
                    act.wait_ge(tw_ready, e)
                    for j in range(2):
                        last = act.activation(osb[kk][0:PT, j, :], ps_oa[kk % 2][0:PT, j * D:(j + 1) * D], ACT.Copy,
                                              scale=wgt[kk][0:PT, j:j + 1])
                    last.then_inc(oa_out, 1)

            expert_loop(act, expert)
            n, r = NT // 4, T // 4
            act.wait_ge(added[0], 16 * CAPT * NE // 2)
            for c in range(4):
                act.dma_start(xb[:, n * c:n * c + n, :],
                              acc[0][r * c:r * c + r, :].rearrange("(t p) d -> p t d", p=P)).then_inc(f_in[c], 16)
            act.wait_ge(ov_stored, 16)
            total = act.value_load(over_table[0:1, 3:4], min_val=0, max_val=MAX_OVER)
            with act.If(total > 0):
                with act.Fori(0, total) as t:
                    act.wait_ge(v_gu, t + 1)
                    act.activation(sg[0][:, 0:P], ps_g[:, 0:P], ACT.Silu).then_inc(v_sg, 1)

        @block.vector
        def _(dve):
            dve.memset(pad_rows[:, :, :].rearrange("p a b -> p (a b)"), 0.0).then_inc(pad_link, 1)
            for t in vt:
                dve.memset(t[:, :, :, :].rearrange("p a b c -> p (a b c)"), 0.0)
            dve.memset(ones_b[:, :], 1.0)
            dve.memset(onese[:, :], 1.0)
            dve.memset(seen[:, :], 0.0)

            def stats(half, src):
                carry_wait(dve)
                for t in range(QT):
                    last = dve.bn_stats(st6[:, half * QT + t, :], src(t))
                last.then_inc(st_done[half], 1)

            def chain(n, halves, part):
                at = [n * LN_LINKS + (0, LN_CUT, LN_CUT + 3)[part]]
                lo, hi = QT * halves[0], QT * (halves[-1] + 1)
                cols = slice(lo, hi)

                def linked(ins):
                    ins.then_inc(ln_link, 1)
                    at[0] = at[0] + 1
                    dve.wait_ge(ln_link, at[0])

                def newton():
                    linked(dve.tensor_tensor(tn[:, cols], rs[:, cols], rs[:, cols], ALU.mult))
                    linked(dve.tensor_tensor(tn[:, cols], tn[:, cols], hv[:, cols], ALU.mult))
                    linked(dve.scalar_tensor_tensor(rs[:, cols], tn[:, cols], 1.5, rs[:, cols], ALU.add, ALU.mult))

                if part == 0:
                    carry_wait(dve)
                    for c in range(lo, hi):
                        last = dve.bn_aggr(mv[:, c, :], st6[:, c, :])
                    linked(last)
                    dve.tensor_scalar(hv[:, cols], mv[:, cols, 1], EPS, -0.5, ALU.add, ALU.mult)
                    linked(dve.tensor_scalar(ve[:, cols], mv[:, cols, 1], EPS, None, ALU.add))
                    linked(dve.tensor_scalar(rs[:, cols].bitcast(i32), ve[:, cols].bitcast(i32), -0.5,
                                             float(RSQRT_MAGIC), ALU.mult, ALU.add))
                newton()

            def apply(half, src, dst, done):
                for t in range(QT):
                    c = half * QT + t
                    last = dve.tensor_scalar(dst[:, t, :], src(t), mv[:, c, 0:1], rs[:, c:c + 1],
                                             ALU.subtract, ALU.mult)
                last.then_inc(done, 1)

            def rows_of(x, b):
                return lambda t: x[:, b * QT + t, :]

            def norm1(b):
                stats(0, rows_of(xall, b))
                wait(dve, st_done[0], b + 1)
                chain(b, [0], 0)
                chain(b, [0], 1)
                chain(b, [0], 2)
                apply(0, rows_of(xall, b), xn, xn_ready)

            dve.wait_ge(s_x0, 16)
            norm1(0)
            dve.wait_ge(s_cst, 32)
            dve.wait_ge(pad_link, 1)
            dve.tensor_copy(pad_rows[:, :, IDC].bitcast(i32), idt[:, 0:CAPT]).then_inc(s_padrow, 1)
            for dst, at in ((ident_b, C_ID), (before_b, C_LT), (causal_b, C_CAUSAL)):
                last = dve.tensor_copy(dst[:, :], cst[:, at:at + P])
            last.then_inc(s_prep, 1)
            dve.tensor_copy(rows[:, :, IDC].bitcast(i32), idt[:, CAPT:CAPT + NT])
            dve.wait_ge(s_w, 16 * 8)
            dve.tensor_copy(bvw[:, :, :], bvs[:, :].unsqueeze(2).broadcast_to([P, DC, P])).then_inc(bvw_ready, 1)

            def rest(i, b):
                wait(dve, qkh_ready[i], b + 1)
                dve.tensor_tensor(qkp[i][:, 1, :], qkT[i][:, :], qkp[i][:, 0, :].bitcast(fp32), ALU.subtract)\
                    .then_inc(qkl_ready[i], 1)

            def rest_of(parts_, ps, rounded, done, value):
                wait(dve, rounded, value)
                dve.tensor_tensor(parts_[1][:, :, :].rearrange("p a b -> p (a b)"), ps[:, :],
                                  parts_[0][:, :, :].rearrange("p a b -> p (a b)").bitcast(fp32), ALU.subtract)\
                    .then_inc(done, 1)

            rest_of(xnT, ps_x0, xnTh_ready, xnT_ready, 1)
            rest(0, 0)
            rest(1, 0)
            dve.wait_ge(xnT_ps, 1)
            dve.wait_ge(s_xrest, 16)
            norm1(1)
            dve.wait_ge(bias_ps, 1)
            dve.tensor_tensor(bos[:, :], ps_s1[0][:, 0:D], bos[:, :], ALU.add).then_inc(bias_ready, 1)

            def step(b, par, n):
                now, pre, post, old = n < NB, n < NB - 1, 1 <= n <= NB, n >= 2
                next_ = n < NB - 2
                halves = [0] * next_ + [1] * post
                for s in range(PAIRS):
                    u = unit(b, s)
                    if s == 2 and post:
                        wait(dve, av_done, b * PAIRS)
                        wait(dve, rdenT_ready, b)
                        wait(dve, wo_ps, b - 1)
                        dve.tensor_tensor(aT[:, :, :].rearrange("p m q -> p (m q)"), ps_o[:, :],
                                          rdenT[:, :, :].rearrange("p m q -> p (m q)"), ALU.mult).then_inc(aT_ready, 1)
                    if now:
                        wait(dve, s1_done, u + 1)
                        dve.reduce_max(nm[:, s % 2, 0:2], ps_s1[s % 2][:, :].rearrange("p (h k) -> p h k", h=2),
                                       axis=AX.X, negate=True).then_inc(nm1_ready, 1)
                        wait(dve, s0_done, u + 1)
                        dve.reduce_max(nm[:, s % 2, 2:4], ps_s0[:, 0:2 * P].rearrange("p (h k) -> p h k", h=2),
                                       axis=AX.X, negate=True).then_inc(nm0_ready, 1)
                    if (now and (n, s) != (0, 0)) or (n == NB and s == 0):
                        wait(dve, t_done[0], u)
                        wait(dve, av_done, u - 2)
                        dve.tensor_copy(pt[0][(s - 1) % 2][:, :], ps_t[0][:, 0:3 * P]).then_inc(pt_ready[0], 1)
                    if s == 1 and pre:
                        rest_of(xnT, ps_x0, xnTh_ready, xnT_ready, b + 2)
                    if s == 0 and post:
                        wait(dve, p0_ready, b * PAIRS)
                        wait(dve, rdenw_ready, b - 1)
                        dve.reciprocal(rden[:, :, :], den[1 - par][:, :, :]).then_inc(rden_ready, 1)
                    if s == 0 and old:
                        wait(dve, lg_ps, b - 1)
                        dve.tensor_copy(lg[:, :, :].rearrange("p a b -> p (a b)"), ps_x1[:, 0:QT * NE]).then_inc(lg_read, 1)
                        wait(dve, lg_read, b - 1)
                        carry_wait(dve)
                        for t in range(QT):
                            last = dve.max(top[:, t, :], lg[:, t, :])
                        last.then_inc(top_link, 1)
                        wait(dve, top_link, b * 2 - 3)
                        dve.tensor_scalar(nmx[:, :], top[:, :, 0], -1.0, None, ALU.mult)
                        for t in range(QT):
                            last = dve.match_replace(others[:, t, :], top[:, t, :], lg[:, t, :], -3e38)
                        last.then_inc(top_link, 1)
                        wait(dve, top_link, b * 2 - 2)
                        dve.tensor_tensor(chosen[:, :, :], others[:, :, :], lg[:, :, :], ALU.is_lt).then_inc(mask_ready, 1)
                    if s == 1 and next_:
                        stats(0, rows_of(xall, b + 2))
                    if s in (2, 3) and pre:
                        rest(s - 2, b + 1)
                    if s == 3 and old:
                        wait(dve, rank_ps, b - 1)
                        dve.tensor_tensor(place[:, :, :], ps_x1[:, 0:QT * NE].rearrange("p (t e) -> p t e", e=NE),
                                          cst[:, C_BASE:C_BASE + NE].unsqueeze(1).broadcast_to([P, QT, NE]),
                                          ALU.add).then_inc(rank_read, 1)
                        dve.tensor_tensor(seen[:, :], seen[:, :], chosen[:, 0, :], ALU.add).then_inc(sl_link, 1)
                        wait(dve, rank_read, b - 1)
                        dve.tensor_tensor(place[:, :, :], place[:, :, :], chosen[:, :, :], ALU.mult).then_inc(sl_link, 1)
                        wait(dve, sl_link, b * 3 - 5)
                        dve.tensor_tensor(seen[:, :], seen[:, :], chosen[:, 1, :], ALU.add)
                        wait(dve, sl_link, b * 3 - 4)
                        carry_wait(dve)
                        for t in range(QT):
                            last = dve.max(slotf[:, t, :], place[:, t, :])
                        last.then_inc(sl_link, 1)
                        wait(dve, sl_link, b * 3 - 3)
                        dve.tensor_scalar(slots[:, bass.ds((b - 2) * QT, QT), :], slotf[:, :, :], -1.0, None,
                                          ALU.add).then_inc(slots_ready, 1)
                    if s == 4 and post:
                        wait(dve, wo_ps, b)
                        wait(dve, xb_ready, b)
                        mine = xb[:, bass.ds((b - 1) * QT, QT), :]
                        dve.tensor_tensor(mine, ps_x0[:, :].rearrange("p (t d) -> p t d", d=D), mine, ALU.add)\
                            .then_inc(x2_ready, 1)
                    if s == 4 and post:
                        wait(dve, x2_ready, b)
                        stats(1, rows_of(xb, b - 1))
                    if s == 4 and old:
                        wait(dve, e_ready, b - 1)
                        dve.reciprocal(erec[:, :], esum[:, :]).then_inc(pr_link, 1)
                        wait(dve, pr_link, b - 1)
                        for t in range(QT):
                            last = dve.tensor_scalar(rows[:, (b - 2) * QT + t, PRC:RW], elg[:, t, :], erec[:, t:t + 1],
                                                     None, ALU.mult)
                        last.then_inc(probs_ready, 1)
                    if s == 5 and halves:
                        if next_:
                            wait(dve, st_done[0], b + 3)
                        if post:
                            wait(dve, st_done[1], b)
                        chain(b + 2, halves, 0)
                        chain(b + 2, halves, 1)
                    if s == 6 and halves:
                        chain(b + 2, halves, 2)
                        if post:
                            wait(dve, x2T_ps, b - 1)
                            wait(dve, rowx_ready, b - 1)
                            apply(1, rows_of(xb, b - 1), xn2, xn2_ready)
                    if s == 7 and next_:
                        wait(dve, xnT_ps, b + 2)
                        apply(0, rows_of(xall, b + 2), xn, xn_ready)

            batches(dve, step)

            links = [0]

            def linked(ins):
                ins.then_inc(ov_link, 1)
                links[0] += 1
                dve.wait_ge(ov_link, links[0])

            dve.wait_ge(cnt_ps, 1)
            linked(dve.tensor_copy(cnt[:, :], ps_x0[:, 0:NE]))
            linked(dve.tensor_tensor(gt[:, :, :], cnt[:, :].unsqueeze(2).broadcast_to([P, NE, OVT]),
                                     cst[:, C_THR:C_THR + OVT].unsqueeze(1).broadcast_to([P, NE, OVT]), ALU.is_gt))
            linked(dve.reduce_sum(nov[:, :], gt[:, :, :], axis=AX.X))
            linked(dve.tensor_tensor_scan(cum[:, :], onese[:, :], nov[:, :], 0.0, ALU.mult, ALU.add))
            linked(dve.tensor_scalar(ge[:, :], cum[:, :], cst[:, C_IOTA:C_IOTA + 1], None, ALU.is_le))
            dve.reduce_sum(ovv[:, 1:2], ge[:, :], axis=AX.X)
            linked(dve.tensor_tensor(ge[:, :], ge[:, :], nov[:, :], ALU.mult))
            linked(dve.reduce_sum(ovv[:, 4:5], ge[:, :], axis=AX.X))
            linked(dve.tensor_scalar(eq[:, :], cst[:, C_EIDX:C_EIDX + NE], ovv[:, 1:2], None, ALU.is_equal))
            linked(dve.tensor_tensor(eq[:, :], eq[:, :], cnt[:, :], ALU.mult))
            linked(dve.reduce_sum(ovv[:, 5:6], eq[:, :], axis=AX.X))
            linked(dve.tensor_tensor(ovv[:, 6:7], cst[:, C_IOTA:C_IOTA + 1], ovv[:, 4:5], ALU.subtract))
            linked(dve.tensor_scalar(ovv[:, 6:7], ovv[:, 6:7], float(P), float(CAP), ALU.mult, ALU.add))
            linked(dve.scalar_tensor_tensor(ovv[:, 0:1], ovv[:, 1:2], float(REG), ovv[:, 6:7], ALU.mult, ALU.add))
            linked(dve.scalar_tensor_tensor(ovv[:, 2:3], ovv[:, 1:2], float(REG), ovv[:, 5:6], ALU.mult, ALU.add))
            linked(dve.tensor_copy(ovv[:, 3:4], cum[:, NE - 1:NE]))
            dve.tensor_copy(ovi[:, :], ovv[:, 0:4]).then_inc(ov_ready, 1)

            def x_out(q, k):
                for c in range(DC):
                    dve.wait_ge(xh_ready[c], q * 4 + k + 1)
                    dve.tensor_tensor(xlo[k % 2][:, c, :], ps_tx[c][:, 0:CAP], xhi[k % 2][:, c, :].bitcast(fp32),
                                      ALU.subtract).then_inc(xl_ready[c], 1)

            def w_out(q, k):
                dve.wait_ge(wh_ready, q * 4 + k + 1)
                dve.tensor_tensor(wlo[k][:, :], wexp[k][:, :], whi[k][:, :].bitcast(fp32),
                                  ALU.subtract).then_inc(wl_ready, 1)

            x_out(0, 0)
            w_out(0, 0)
            w_out(0, 1)

            def expert(q, k, n):
                e = q * 4 + k
                if n < NE - 1:
                    x_out(*after(q, k))
                if n < NE:
                    dve.wait_ge(sg_ready, e + 1)
                    dve.wait_ge(u_ps, e + 1)
                    dve.tensor_tensor(hT[k % 2][:, :], sg[k % 2][:, :], ps_u[:, 0:CAP], ALU.mult).then_inc(h_ready, 1)
                    if n >= 4:
                        dve.wait_ge(added[k % 2], earlier_adds(q - 1, k) + 16 * CAPT)
                    if n < NE - 2:
                        w_out(*after(*after(q, k)))
                    dve.wait_ge(hh_ready, e + 1)
                    dve.tensor_tensor(hlo[k % 2][:, :], hT[k % 2][:, :], hhi[k % 2][:, :].bitcast(fp32),
                                      ALU.subtract).then_inc(hl_ready, 1)
                    dve.tensor_copy(tok[k][0:PT, :], xt[k][0:PT, :, IDC].bitcast(i32))
                    dve.tensor_copy(wgt[k][0:PT, :], xt[k][0:PT, :, bass.ds(e + PRC, 1)].rearrange("p j o -> p (j o)"))\
                        .then_inc(tw_ready, 1)
                if n > 0:
                    kk = (k - 1) % 4
                    dve.wait_ge(tw_ready, e)
                    dve.wait_ge(ob_ps, e)
                    dve.tensor_scalar(osb[kk][0:PT, 2, :], ps_ob[kk % 2][0:PT, 0:D],
                                      wgt[kk][0:PT, 2:3], None, ALU.mult).then_inc(ob_out, 1)

            expert_loop(dve, expert)

            dve.wait_ge(ov_stored, 16)
            total = dve.value_load(over_table[0:1, 3:4], min_val=0, max_val=MAX_OVER)
            with dve.If(total > 0):
                with dve.Fori(0, total) as t:
                    e = dve.value_load(over_table[bass.ds(t, 1), 1:2], min_val=0, max_val=NE - 1)
                    dve.wait_ge(v_tx, t + 1)
                    for c in range(DC):
                        last = dve.tensor_copy(xT[:, c, :], ps_tx[c][:, 0:P])
                    last.then_inc(v_xT, 1)
                    dve.wait_ge(v_sg, t + 1)
                    dve.tensor_tensor(hT[0][:, 0:P], sg[0][:, 0:P], ps_u[:, 0:P], ALU.mult).then_inc(v_h, 1)
                    dve.wait_ge(added[0], 16 * CAPT * NE // 2)
                    dve.wait_ge(v_o, t + 1)
                    dve.tensor_scalar(osb[0][:, 0, :], ps_oa[0][:, 0:D], xt[0][:, 0, bass.ds(e + PRC, 1)], None,
                                      ALU.mult).then_inc(v_osb, 1)

            for c in range(4):
                n = NT // 4
                mine = xb[:, n * c:n * c + n, :]
                dve.wait_ge(f_in[c], 32)
                dve.tensor_tensor(mine, mine, rows[:, n * c:n * c + n, 0:D], ALU.add).then_inc(f_sum, 1)


def kernel(**inputs):
    import concourse.bacc as bacc
    from concourse import mybir as mb
    from concourse.bass_utils import run_bass_kernel_spmd

    a = {k: np.asarray(v) for k, v in inputs.items()}
    w13, w2 = a["L0_ffn_w13"], a["L0_ffn_w2"]
    w13t = np.transpose(w13.reshape(NE, 2 * INTER, DC, P), (0, 3, 2, 1)).reshape(NE, P, DC * 2 * INTER)
    experts = np.concatenate([w13t, np.transpose(w2, (0, 2, 1))], axis=2)
    bq, bk = a["L0_attn_bq"].reshape(DC, P), a["L0_attn_bk"].reshape(DC, P)
    p = np.arange(P)
    consts = np.zeros((P, C_END), np.float32)
    consts[:, C_ID:C_ID + P] = np.eye(P)
    consts[:, C_LT:C_LT + P] = p[:, None] < p[None, :]
    consts[:, C_CAUSAL:C_CAUSAL + P] = np.where(p[None, :] > p[:, None], LOW, 0.0)
    consts[:, C_BASE:C_BASE + NE] = np.arange(NE) * REG + 1
    consts[:, C_EIDX:C_EIDX + NE] = np.arange(NE)
    consts[:, C_IOTA] = p
    consts[:, C_THR:C_THR + OVT] = CAP + P * np.arange(OVT)
    ids = np.concatenate([T + p[:, None] + P * np.arange(CAPT), p[:, None] + P * np.arange(NT)], axis=1)
    arrays = {
        "x": a["L0_attn_x"].reshape(T, D),
        "wq": a["L0_attn_wq"].T, "wk": a["L0_attn_wk"].T, "wv": a["L0_attn_wv"].T, "wo": a["L0_attn_wo"].T,
        "bqk": np.stack([*bq, *bk], axis=1), "bv": np.stack([*a["L0_attn_bv"].reshape(DC, P)], axis=1), "bo": a["L0_attn_bo"][None, :],
        "gate": a["L0_ffn_gate_w"].T, "experts": experts, "consts": consts, "ids": ids.astype(np.int32),
    }
    arrays = {k: np.ascontiguousarray(v) for k, v in arrays.items()}
    nc = bacc.Bacc("TRN2", target_bir_lowering=False, num_devices=1)
    args = {k: nc.dram_tensor(k + "_dram", v.shape, mb.dt.from_np(v.dtype), kind="ExternalInput").ap()
            for k, v in arrays.items()}
    args["y"] = nc.dram_tensor("y_dram", (T, D), mb.dt.float32, kind="ExternalOutput").ap()
    program(nc, **args)
    r = run_bass_kernel_spmd(nc, [{k + "_dram": v for k, v in arrays.items()}], core_ids=[0])
    return r.results[0]["y_dram"].reshape(NB, SEQ, D)
```
